# Optimizing a Trainium2 kernel written in Bass

```python
import numpy as np
import jax
import jax.numpy as jnp

def _softmax(x, axis=-1):
    return jax.nn.softmax(x, axis=axis)

def _gelu(x):
    return jax.nn.gelu(x, approximate=True)

def _silu(x):
    return jax.nn.silu(x)

def _sigmoid(x):
    return jax.nn.sigmoid(x)

def _layernorm(x, axis=-1, eps=1e-05):
    m = jnp.mean(x, axis=axis, keepdims=True)
    v = jnp.var(x, axis=axis, keepdims=True)
    return (x - m) / jnp.sqrt(v + eps)

def _scatter_add(tgt, idx, src, axis=0):
    return tgt.at[idx].add(src)

def _segment_sum(src, seg, n):
    return jax.ops.segment_sum(src, seg, n)
kernel_name = 'mk_macaron_d1_jaxref_r8_4b6b0a'

def setup_inputs(seed: int=0):
    np.random.seed(seed)
    _w = jnp.asarray

    def _L0_attn_setup():
        import jax, jax.numpy as jnp
        import numpy as np
        import math
        D_MODEL = 256
        NUM_HEAD = 16
        HEAD_DIM = D_MODEL // NUM_HEAD

        def _trunc_normal(key, shape, std):
            return jax.random.truncated_normal(key, -3.0, 3.0, shape, dtype=jnp.float32) * std
        key = jax.random.key(seed)
        kx, kp, ko = jax.random.split(key, 3)
        b, s = (4, 256)
        x = jax.random.normal(kx, (b, s, D_MODEL), dtype=jnp.float32)
        sigma_p = math.sqrt(2.0 / (D_MODEL + 3 * D_MODEL))
        w_project = _trunc_normal(kp, (3 * D_MODEL, D_MODEL), sigma_p)
        sigma_o = math.sqrt(2.0 / (D_MODEL + D_MODEL))
        w_out = _trunc_normal(ko, (D_MODEL, D_MODEL), sigma_o)
        return {'x': x, 'w_project': w_project, 'w_out': w_out}
    _L0_attn_in = _L0_attn_setup()

    def _L0_ffn_setup():
        import jax, jax.numpy as jnp
        import numpy as np
        BLOCK_SIZE = 32
        HIDDEN_SIZE = 256
        MLP_DIM = 2048
        NVFP4_LUT = jnp.array([0.0, 0.5, 1.0, 1.5, 2.0, 3.0, 4.0, 6.0, 0.0, -0.5, -1.0, -1.5, -2.0, -3.0, -4.0, -6.0], dtype=jnp.float32)

        def dequant_nvfp4(W_packed, scales, block=BLOCK_SIZE):
            N = W_packed.shape[0]
            low = W_packed & 15
            high = W_packed >> 4 & 15
            idx = jnp.stack([low, high], axis=-1).reshape(N, -1)
            vals = NVFP4_LUT[idx]
            K = vals.shape[1]
            vals = vals.reshape(N, K // block, block) * scales[:, :, None]
            return vals.reshape(N, K)
        key = jax.random.key(seed)
        ks = jax.random.split(key, 7)
        x = jax.random.normal(ks[0], (4, 32, HIDDEN_SIZE), dtype=jnp.float32)
        gate_W_packed = jax.random.randint(ks[1], (MLP_DIM, HIDDEN_SIZE // 2), 0, 32, dtype=jnp.int32)
        gate_scales = jax.random.uniform(ks[2], (MLP_DIM, HIDDEN_SIZE // BLOCK_SIZE), dtype=jnp.float32) * 0.1 + 0.001
        up_W_packed = jax.random.randint(ks[3], (MLP_DIM, HIDDEN_SIZE // 2), 0, 32, dtype=jnp.int32)
        up_scales = jax.random.uniform(ks[4], (MLP_DIM, HIDDEN_SIZE // BLOCK_SIZE), dtype=jnp.float32) * 0.1 + 0.001
        down_W_packed = jax.random.randint(ks[5], (HIDDEN_SIZE, MLP_DIM // 2), 0, 32, dtype=jnp.int32)
        down_scales = jax.random.uniform(ks[6], (HIDDEN_SIZE, MLP_DIM // BLOCK_SIZE), dtype=jnp.float32) * 0.1 + 0.001
        return {'x': x, 'gate_W_packed': gate_W_packed, 'gate_scales': gate_scales, 'up_W_packed': up_W_packed, 'up_scales': up_scales, 'down_W_packed': down_W_packed, 'down_scales': down_scales}
    _L0_ffn_in = _L0_ffn_setup()
    _d = {'L0_attn_x': _L0_attn_in['x'], 'L0_attn_w_project': _L0_attn_in['w_project'], 'L0_attn_w_out': _L0_attn_in['w_out'], 'L0_ffn_gate_W_packed': _L0_ffn_in['gate_W_packed'], 'L0_ffn_gate_scales': _L0_ffn_in['gate_scales'], 'L0_ffn_up_W_packed': _L0_ffn_in['up_W_packed'], 'L0_ffn_up_scales': _L0_ffn_in['up_scales'], 'L0_ffn_down_W_packed': _L0_ffn_in['down_W_packed'], 'L0_ffn_down_scales': _L0_ffn_in['down_scales']}
    _x0 = _d['L0_attn_x']
    _d['L0_attn_x'] = jax.random.normal(jax.random.fold_in(jax.random.key(seed), 1), (1, 2048, 256), dtype=_x0.dtype)
    del _x0
    return _d

def reference(L0_attn_x, L0_attn_w_project, L0_attn_w_out, L0_ffn_gate_W_packed, L0_ffn_gate_scales, L0_ffn_up_W_packed, L0_ffn_up_scales, L0_ffn_down_W_packed, L0_ffn_down_scales):

    def _L0_attn_ref(x, w_project, w_out):
        import jax, jax.numpy as jnp
        import numpy as np
        import math
        D_MODEL = 256
        NUM_HEAD = 16
        HEAD_DIM = D_MODEL // NUM_HEAD

        def _trunc_normal(key, shape, std):
            return jax.random.truncated_normal(key, -3.0, 3.0, shape, dtype=jnp.float32) * std
        b, s, d = x.shape
        qkv = jnp.einsum('bsd,od->bso', x, w_project)
        qkv = qkv.reshape(b, s, 3, NUM_HEAD, HEAD_DIM)
        qkv = jnp.transpose(qkv, (2, 0, 3, 1, 4))
        q, k, v = (qkv[0], qkv[1], qkv[2])
        att = jnp.einsum('bhqd,bhkd->bhqk', q, k) / math.sqrt(HEAD_DIM)
        causal = jnp.triu(jnp.ones((s, s), dtype=bool), k=1)
        att = jnp.where(causal[None, None, :, :], jnp.float32(-1000000000.0), att)
        att = jax.nn.softmax(att, axis=-1)
        out = jnp.einsum('bhqk,bhkd->bhqd', att, v)
        out = jnp.transpose(out, (0, 2, 1, 3)).reshape(b, s, d)
        return jnp.einsum('bsd,od->bso', out, w_out)

    def _L0_ffn_ref(x, gate_W_packed, gate_scales, up_W_packed, up_scales, down_W_packed, down_scales):
        import jax, jax.numpy as jnp
        import numpy as np
        BLOCK_SIZE = 32
        HIDDEN_SIZE = 256
        MLP_DIM = 2048
        NVFP4_LUT = jnp.array([0.0, 0.5, 1.0, 1.5, 2.0, 3.0, 4.0, 6.0, 0.0, -0.5, -1.0, -1.5, -2.0, -3.0, -4.0, -6.0], dtype=jnp.float32)

        def dequant_nvfp4(W_packed, scales, block=BLOCK_SIZE):
            N = W_packed.shape[0]
            low = W_packed & 15
            high = W_packed >> 4 & 15
            idx = jnp.stack([low, high], axis=-1).reshape(N, -1)
            vals = NVFP4_LUT[idx]
            K = vals.shape[1]
            vals = vals.reshape(N, K // block, block) * scales[:, :, None]
            return vals.reshape(N, K)
        B, S, H = x.shape
        xt = x.reshape(B * S, H)
        Wg = dequant_nvfp4(gate_W_packed, gate_scales)
        Wu = dequant_nvfp4(up_W_packed, up_scales)
        Wd = dequant_nvfp4(down_W_packed, down_scales)
        gate = jnp.einsum('th,nh->tn', xt, Wg)
        up = jnp.einsum('th,nh->tn', xt, Wu)
        gelu = jnp.tanh(0.7978845608028654 * (gate + 0.044715 * gate ** 3)) * gate * 0.5 + gate * 0.5
        inter = gelu * up
        out = jnp.einsum('tn,hn->th', inter, Wd)
        return out.reshape(B, S, H)
    x = L0_attn_x
    x = x + 0.5 * _L0_ffn_ref(_layernorm(x, axis=-1), L0_ffn_gate_W_packed, L0_ffn_gate_scales, L0_ffn_up_W_packed, L0_ffn_up_scales, L0_ffn_down_W_packed, L0_ffn_down_scales)
    x = x + _L0_attn_ref(_layernorm(x, axis=-1), L0_attn_w_project, L0_attn_w_out)
    x = x + 0.5 * _L0_ffn_ref(_layernorm(x, axis=-1), L0_ffn_gate_W_packed, L0_ffn_gate_scales, L0_ffn_up_W_packed, L0_ffn_up_scales, L0_ffn_down_W_packed, L0_ffn_down_scales)
    return x

_drawn_inputs = setup_inputs


def setup_inputs(seed=0):
    import zlib

    import numpy as np

    out = dict(_drawn_inputs(seed))
    spreads = {}
    factors = {'L0_attn_w_project': 4.753, 'L0_attn_w_out': 4.92}
    for name, (base, spread) in spreads.items():
        noise = np.random.default_rng([zlib.crc32(name.encode()), seed]).standard_normal(out[name].shape)
        drawn = base * np.exp(spread * noise) if base else spread * noise
        out[name] = jnp.asarray(drawn.astype(out[name].dtype))
    for name, factor in factors.items():
        out[name] = (out[name] * factor).astype(out[name].dtype)
    return out
```

```python
import concourse.bass as bass
from concourse import mybir
from contextlib import ExitStack


def macaron_block(nc, x, w_project, w_out, gate_packed, gate_scales, up_packed, up_scales,
                  down_packed, down_scales, out):
    f32, f16, i32 = mybir.dt.float32, mybir.dt.float16, mybir.dt.int32
    ALU, ACT, AX = mybir.AluOpType, mybir.ActivationFunctionType, mybir.AxisListType

    P = 128
    T, D = x.shape[1], x.shape[2]
    F = gate_packed.shape[0]
    BLK = D // gate_scales.shape[1]
    HEADS, HD = 16, D // 16
    TT = T // P
    CT = 512
    NCH = T // CT
    TPC = CT // P
    NT = F // P
    KT = D // P
    NJ = NT // 2
    EPS = 1e-5
    GH = 4
    NG = HEADS // GH
    NPAIR = HEADS // 2
    BIG = 30000.0
    MSCALE = 256.0
    MSCALE_PAIR = 0x5C005C00
    EXP_SCALE = float(HD) ** -0.5

    X_POW, W_POW, P_POW, V_POW = 11, 12, 14, 6
    I_POW = -8
    FP4_POW = 14

    ctx = ExitStack()
    with ctx:
        def sb(name, shape, dt):
            return ctx.enter_context(nc.sbuf_tensor(name, shape, dt))

        def sem(name):
            return ctx.enter_context(nc.semaphore(name))

        xres = sb("xres", [P, TT * D], f32)
        yn = sb("yn", [P, TPC, D], f32)
        xT = sb("xT", [P, 2, KT, CT], f16)
        wg = sb("wg", [P, 2, KT, F], f16)
        wu = sb("wu", [P, 2, KT, F], f16)
        wd = sb("wd", [P, NT, 2 * D], f16)
        wp = sb("wp", [P, 2, KT, 3 * D], f16)
        wo = sb("wo", [P, KT, 2 * D], f16)
        v1 = sb("v1", [P, TT, HEADS, HD + 1], f32)
        ident = sb("ident", [P, P], f32)
        big_id = sb("big_id", [P, 64], f16)
        tri_a = sb("tri_a", [P, 2, P], f16)
        tri_b = sb("tri_b", [P, 2, P], f16)
        sg = sb("sg", [P, NT, D // BLK], f32)
        su = sb("su", [P, NT, D // BLK], f32)
        sd = sb("sd", [P, KT, F // BLK], f32)
        amax = sb("amax", [P, 5], f32)
        amax_all = sb("amax_all", [P, 5], f32)
        pow_r = sb("pow_r", [P, 5], f32)
        pow_i = sb("pow_i", [P, 5], f32)
        mul_w = sb("mul_w", [P, 5], f32)
        gelu_in = sb("gelu_in", [P, 1], f32)
        kappa = sb("kappa", [P, 1], f32)
        s_down = sb("s_down", [P, 1], f32)
        s_qk = sb("s_qk", [P, 1], f32)
        s_out = sb("s_out", [P, 1], f32)
        tmp1 = sb("tmp1", [P, 1], f32)
        stats = sb("stats", [P, TPC, 6], f32)
        mv = sb("mv", [P, TPC, 2], f32)
        neg_mean = sb("neg_mean", [P, TPC], f32)
        rstd = sb("rstd", [P, TPC], f32)
        minus_half = sb("minus_half", [P, TPC], f32)
        half_sum = sb("half_sum", [P, 2, D], f32)
        m_part = sb("m_part", [P, 2, 2, 16], f32)
        m_split = sb("m_split", [P, 2, 2, 2, 8], f16)
        m_rows = sb("m_rows", [32, 2, P], f16)
        ident16 = sb("ident16", [P, P], f16)
        att = sb("att", [P, 2, D], f32)
        attT = sb("attT", [P, 2, 2, KT, P], f16)
        recip = sb("recip", [P, 2, HEADS], f32)

        qreg = sb("qreg", [P, NCH, NPAIR, CT], f16)
        kreg = sb("kreg", [P, NPAIR, T], f16)
        wreg = sb("wreg", [P, 8, CT], f32)
        qflat = qreg[:, :, :, :].rearrange("p c a t -> p (c a t)")
        inter = qflat.rearrange("p (s n t) -> p s n t", s=2, n=NT)
        kflat = kreg[:, :, :].rearrange("p a t -> p (a t)").bitcast(i32)
        gate_nat, up_nat, down_nat = (kflat[:, k * 2048:(k + 1) * 2048] for k in range(3))
        proj_nat = kflat[:, 6144:6144 + 1536].bitcast(f32)
        out_nat = kflat[:, 7680:8192].bitcast(f32)
        bits = [[qflat.bitcast(i32)[:, 512 * (3 * k + m):512 * (3 * k + m + 1)] for m in range(3)] for k in range(2)]
        code_pair = [qflat.bitcast(i32)[:, 512 * (6 + k):512 * (7 + k)] for k in range(2)]
        vals = [wreg[:, 2 * k:2 * k + 2, :].rearrange("p a b -> p (a b)") for k in range(4)]
        gelu_ring = wreg[:, 0:3, :]
        prod_ring = wreg[:, 3:6, :]
        qk_flat = wreg[:, :, :].bitcast(f16).rearrange("p a b -> p (a b)")\
            .rearrange("p (r s m t) -> p r s m t", r=2, s=2, m=4)
        oT = qflat.bitcast(f32).rearrange("p (c g t) -> p c g t", c=NCH, g=NG)

        qk_dram = nc.dram_tensor("qk_split", [2, 4, P, T], f16, kind="Internal").ap()
        ps = ctx.enter_context(nc.psum_tensor("ps", [P, 8 * 512], f32))

        def bank(b, n=512, at=0, width=1):
            return ps[:, 512 * b + at:512 * b + at + n]

        s_scales, s_packed = sem("scales_in"), [sem(f"packed_in{k}") for k in range(3)]
        s_proj_in, s_out_in = sem("proj_in"), sem("w_out_in")
        s_x = [sem(f"x_in{k}") for k in range(NCH)]
        s_const = sem("constants")
        s_pool = sem("pool_step")
        s_dve = sem("dve_step")
        s_amax, s_amax_all = sem("amax"), sem("amax_all")
        s_scaled = sem("scales_scaled")
        s_code = sem("codes_decoded")
        s_vals = sem("weights_decoded")
        s_wt = sem("weights_transposed")
        s_wh, s_wl = sem("weights_high"), sem("weights_low")
        s_stats, s_yn = sem("stats_ready"), sem("normalised")
        s_xt, s_xh, s_xl = sem("x_transposed"), sem("xT_high"), sem("xT_low")
        s_gate, s_up = sem("gate_products"), sem("up_products")
        s_gelu, s_prod = sem("gelu_done"), sem("product_done")
        s_ihigh, s_inter = sem("inter_high"), sem("inter_ready")
        s_down_done, s_half, s_resid = sem("down_products"), sem("residual_half"), sem("residual_done")
        s_qk_ps, s_v_ps = sem("qk_products"), sem("v_products")
        s_qkh, s_qkl, s_v = sem("qk_high"), sem("qk_low"), sem("v_ready")
        s_qk_out, s_ones = sem("qk_in_dram"), sem("key_ones")
        s_stack = [sem(f"stacks_in{k}") for k in range(NCH)]
        s_ascore, s_aread = sem("max_scores"), sem("max_scores_read")
        s_mneg = sem("maxima_ready")
        s_mdma = [sem("max_rows_in0"), sem("max_rows_in1")]
        s_score, s_p, s_pv, s_o = sem("scores"), sem("probs"), sem("pv_done"), sem("o_read")
        s_onat, s_att, s_attT = sem("o_natural"), sem("att_ready"), sem("att_transposed")
        s_atth, s_attl, s_oproj = sem("att_high"), sem("att_low"), sem("out_products")
        s_oresid = sem("attention_added")
        s_store = sem("stored")

        block = ctx.enter_context(nc.Block())

        NPIECE = 4
        groups = [("gate", j) for j in range(NJ)] + [("up", j) for j in range(NJ)] + \
                 [("down", j) for j in range(NJ)] + [("proj", j) for j in range(3)] + [("out", 0)]
        W_BANKS = 4

        LEAD = 3
        steps = [(NG * c + g, c, g, j) for c in range(NCH) for g in range(NG) for j in range(TPC * (c + 1))]
        first_step = {}
        for t, (n, _, _, _) in enumerate(steps):
            first_step.setdefault(n, t)
        NGRP = NG * NCH

        def max_units(c, g):
            units = []
            for q in range(TPC):
                i = TPC * c + q
                n = P * (i + 1)
                if n <= 512:
                    for h in (0, 2):
                        units.append(([(h, i, 0, n), (h + 1, i, 0, n)], n, (0, q, h, 2)))
                else:
                    for h in range(GH):
                        units.append(([(h, i, 0, min(n, 1024))], min(n, 1024), (0, q, h, 1)))
                    if n > 1536:
                        for h in range(GH):
                            units.append(([(h, i, 1024, n)], n - 1024, (1, q, h, 1)))
                    elif n > 1024:
                        for h in (0, 2):
                            units.append(([(h, i, 1024, n), (h + 1, i, 1024, n)], n - 1024, (1, q, h, 2)))
            return units

        plan = {t: [] for t in range(-1, len(steps))}
        for n in range(NGRP):
            c, g = n // NG, n % NG
            units = [("unit", n, u) for u in max_units(c, g)]
            end = first_step[n] - LEAD
            start = first_step[n - 1] - LEAD if n else end
            for k, u in enumerate(units):
                t = start + (k * (end - start)) // len(units) if n else -1
                plan[max(t, -1)].append(u)
            plan[max(end - 1, -1)].append(("negate", n, None))
            plan[max(end, -1)].append(("rows", n, None))
        k = plan[-1].index(("rows", 0, None))
        plan[-1][k:k + 4] = plan[-1][k + 1:k + 4] + [plan[-1][k]]
        QKV_GROUPS = 4 + TPC

        def early_units(k):
            n = len(plan[-1])
            return plan[-1][n * k // QKV_GROUPS:n * (k + 1) // QKV_GROUPS]

        in_slots = [(kind, n) for t in sorted(plan) for kind, n, _ in plan[t] if kind != "negate"]
        rows_written = {n: k + 1 for k, (kind, n) in enumerate(in_slots) if kind == "rows"}

        @block.sync
        def _(sp):
            sp.dma_start(sg[:, :, :].rearrange("p (j two) b -> p j (two b)", two=2),
                         gate_scales.rearrange("(j p two) b -> p j (two b)", p=P, two=2)).then_inc(s_scales, 16)
            sp.dma_start(su[:, :, :].rearrange("p (j two) b -> p j (two b)", two=2),
                         up_scales.rearrange("(j p two) b -> p j (two b)", p=P, two=2)).then_inc(s_scales, 16)
            sp.dma_start(sd[:, :, :], down_scales.rearrange("(k p) b -> p k b", p=P)).then_inc(s_scales, 16)
            sp.dma_start(proj_nat.rearrange("p (m d) -> p m d", d=D),
                         w_project.rearrange("(m p) d -> p m d", p=P)).then_inc(s_proj_in, 16)
            sp.dma_start(out_nat.rearrange("p (m d) -> p m d", d=D),
                         w_out.rearrange("(m p) d -> p m d", p=P)).then_inc(s_out_in, 16)
            for k, (dst, src) in enumerate(((gate_nat, gate_packed), (up_nat, up_packed))):
                sp.dma_start(dst.rearrange("p (j r) -> p j r", j=NJ),
                             src.rearrange("(j p two) c -> p j (two c)", p=P, two=2)).then_inc(s_packed[k], 16)
            sp.dma_start(down_nat.rearrange("p (k c) -> p k c", k=KT),
                         down_packed.rearrange("(k p) c -> p k c", p=P)).then_inc(s_packed[2], 16)

            sp.wait_ge(s_ones, 1)
            for c in range(NCH):
                cols = slice(CT * c, CT * (c + 1))
                sp.wait_ge(s_qkl, 4 * c + 4)
                sp.dma_start(qk_dram[:, :, :, cols].rearrange("s m p t -> p s m t"),
                             qk_flat[:, c % 2, :, :, :]).then_inc(s_qk_out, 16)
                sp.wait_ge(s_qk_out, 16 * (c + 1))
                for reg, m0, parts in ((kreg, 2, (0, 0, 1)), (qreg, 0, (0, 1, 0))):
                    for half in range(2):
                        for k, part in enumerate(parts):
                            r = 64 * half + HD * k
                            src = qk_dram[part, m0:m0 + 2, :, cols]\
                                .rearrange("m (p a d) t -> a d (m p) t", a=2, d=HD)[half]
                            dst = kreg[r:r + HD, :, cols] if reg is kreg else qreg[r:r + HD, c, :, :]
                            sp.dma_start(dst, src).then_inc(s_stack[c], 16)

            for n in range(NGRP):
                c, g = n // NG, n % NG
                sp.wait_ge(s_aread, rows_written[n])
                for a in range(2):
                    r = 64 * a + 3 * HD
                    dst = qreg[r:r + 2, c, 2 * g:2 * g + 2, :].rearrange("r a t -> r (a t)")
                    sp.dma_start(dst.rearrange("r (k q) -> r k q", q=P),
                                 m_rows[16 * a:16 * a + 16, n % 2, :]).then_inc(s_mdma[n % 2], 16)

            for c in range(NCH):
                sp.wait_ge(s_resid, 1 + TPC * (NCH + c + 1))
                sp.dma_start(out[0, CT * c:CT * (c + 1), :].rearrange("(n p) d -> p n d", p=P),
                             xres[:, TPC * D * c:TPC * D * (c + 1)].rearrange("p (n d) -> p n d", d=D))\
                  .then_inc(s_store, 16)
            sp.wait_ge(s_store, 16 * NCH)

        def normalise(pool, own, job, chunk):
            pool.wait_ge(s_stats, job + 1)
            own(pool.tensor_scalar(neg_mean[:, :], mv[:, :, 0], -1.0, None, ALU.mult))
            own(pool.tensor_scalar(rstd[:, :], mv[:, :, 1], EPS, 2.0 ** (-2 * X_POW), ALU.add, ALU.mult))
            own(pool.tensor_tensor(rstd[:, :], rstd[:, :], minus_half[:, :], ALU.pow))
            if job:
                pool.wait_ge(s_xt, job)
            for n in range(TPC):
                last = pool.tensor_scalar(yn[:, n, :], xres[:, D * (TPC * chunk + n):D * (TPC * chunk + n + 1)],
                                          neg_mean[:, n:n + 1], rstd[:, n:n + 1], ALU.add, ALU.mult)
            last.then_inc(s_yn, 1)

        @block.gpsimd
        def _(pool):
            step = [0]

            def own(ins):
                ins.then_inc(s_pool, 1)
                step[0] += 1
                pool.wait_ge(s_pool, step[0])

            own(pool.memset(ident[:, :], 0.0))
            pool.affine_select(out=ident[:, :], in_=ident[:, :], compare_op=ALU.not_equal, fill=1.0,
                               base=0, pattern=[[-1, P]], channel_multiplier=1).then_inc(s_const, 1)
            own(pool.memset(minus_half[:, :], -0.5))
            own(pool.memset(ident16[:, :], 0.0))
            own(pool.affine_select(out=ident16[:, :], in_=ident16[:, :], compare_op=ALU.not_equal, fill=1.0,
                                   base=0, pattern=[[-1, P]], channel_multiplier=1))
            pool.wait_ge(s_amax, 1)
            pool.partition_all_reduce(amax_all[:, :], amax[:, :], P, bass.bass_isa.ReduceOp.max)\
                .then_inc(s_amax_all, 1)
            normalise(pool, own, 0, 0)

            pool.wait_ge(s_scaled, 1)
            for m in range(3):
                for q in range(NPIECE):
                    n = NPIECE * m + q
                    pool.wait_ge(s_code, n + 1)
                    if n >= 4:
                        pool.wait_ge(s_wt, 2 * (n - 4) + 2)
                    rows = 4 if m < 2 else KT
                    codes = code_pair[n % 2].bitcast(f16).rearrange("p (r j two) -> p r j two", r=rows, two=2)
                    scales = (sg[:, 4 * q:4 * q + 4, :], su[:, 4 * q:4 * q + 4, :], sd[:, :, 16 * q:16 * q + 16])[m]
                    for k in range(2):
                        dst = vals[n % 4].rearrange("p (r k j) -> p r k j", r=rows, k=2)[:, :, k, :]\
                            .rearrange("p r (b e) -> p r b e", e=BLK // 2)
                        last = pool.tensor_tensor(
                            dst, codes[:, :, :, k].rearrange("p r (b e) -> p r b e", e=BLK // 2),
                            scales.unsqueeze(3).to_broadcast(list(dst.shape)), ALU.mult)
                    last.then_inc(s_vals, 1)

            pool.memset(tri_a[:, :, :], -BIG)
            pool.memset(tri_b[:, :, :], -BIG)
            pool.memset(v1[:, :, :, :], 1.0)
            own(pool.memset(big_id[:, :], 0.0))
            for a in range(2):
                half = slice(64 * a, 64 * a + 64)
                pool.affine_select(out=big_id[half, :], in_=big_id[half, :], compare_op=ALU.not_equal, fill=BIG,
                                   base=0, pattern=[[-1, 64]], channel_multiplier=1)
                pool.affine_select(out=tri_a[half, :, :], in_=tri_a[half, :, :], compare_op=ALU.is_gt, fill=0.0,
                                   base=0, pattern=[[64, 2], [-1, P]], channel_multiplier=1)
                last = pool.affine_select(out=tri_b[half, :, :], in_=tri_b[half, :, :], compare_op=ALU.is_gt,
                                          fill=0.0, base=0, pattern=[[-64, 2], [1, P]], channel_multiplier=-1)
            last.then_inc(s_const, 1)
            pool.wait_ge(s_const, 2)

            pool.wait_ge(s_wt, len(groups))
            pool.memset(kflat, MSCALE_PAIR).then_inc(s_ones, 1)
            pool.wait_ge(s_ones, 1)

            for job in range(1, 3 * NCH):
                normalise(pool, own, job, job % NCH)

        def group_banks(k):
            kind, j = groups[k]
            src = bank(k % W_BANKS).rearrange("p (k n) -> p k n", k=KT)
            if kind in ("gate", "up", "proj"):
                w = {"gate": wg, "up": wu, "proj": wp}[kind]
                return src, [w[:, s, :, 256 * j:256 * j + 256] for s in range(2)]
            w, a = (wd, 2 * j) if kind == "down" else (wo, 0)
            return src, [w[:, a:a + 2, D * s:D * s + D] for s in range(2)]

        def down_bank(n):
            return bank(4 + n % 2)

        XT_BANKS = ps[:, 6 * 512:8 * 512].rearrange("p (k t) -> p k t", k=KT)

        def copy_o(act, n, t):
            c, g = n // NG, n % NG
            act.wait_ge(s_pv, t)
            act.activation(oT[:, c, g, :], bank(3), ACT.Copy).then_inc(s_o, 1)

        @block.scalar
        def _(act):
            for k in range(NCH):
                act.dma_start(xres[:, TPC * D * k:TPC * D * (k + 1)].rearrange("p (n d) -> p n d", d=D),
                              x[0, CT * k:CT * (k + 1), :].rearrange("(n p) d -> p n d", p=P)).then_inc(s_x[k], 16)
            act.sem_inc(s_gelu, 1)
            for k in range(len(groups)):
                src, (high, _) = group_banks(k)
                act.wait_ge(s_wt, k + 1)
                act.activation(high, src, ACT.Copy).then_inc(s_wh, 1)

            def x_high(job):
                act.wait_ge(s_xt, job + 1)
                act.activation(xT[:, 0, :, :], XT_BANKS, ACT.Copy).then_inc(s_xh, 1)

            def ffn_chunk(cc, job):
                for n in range(NT):
                    act.wait_ge(s_gate, cc * NT + (n + 1))
                    act.wait_ge(s_prod, cc * NT + (1 if n < 3 else n - 1))
                    act.activation(gelu_ring[:, n % 3, :], bank(n % 2), ACT.Gelu_apprx_tanh,
                                   scale=gelu_in[:, 0:1]).then_inc(s_gelu, 1)
                if job is not None:
                    x_high(job)

            x_high(0)
            with act.Fori(0, NCH - 1) as c:
                ffn_chunk(c, c + 1)
            ffn_chunk(NCH - 1, NCH)

            for c in range(NCH):
                if c >= 2:
                    act.wait_ge(s_qk_out, 16 * (c - 1))
                for m in range(4):
                    act.wait_ge(s_qk_ps, 4 * c + m + 1)
                    act.activation(qk_flat[:, c % 2, 0, m, :], bank(m % 2), ACT.Copy,
                                   scale=s_qk[:, 0:1]).then_inc(s_qkh, 1)
                for n in range(TPC):
                    act.wait_ge(s_v_ps, TPC * c + n + 1)
                    act.activation(v1[:, TPC * c + n, :, 0:HD],
                                   bank(2 + n % 2, D).rearrange("p (h e) -> p h e", e=HD), ACT.Copy,
                                   scale=2.0 ** (V_POW - X_POW - P_POW)).then_inc(s_v, 1)
                if c < NCH - 1:
                    x_high(NCH + c + 1)

            act.wait_ge(s_qk_out, 16 * NCH)
            for t, (n, c, g, j) in enumerate(steps):
                if n and t == first_step[n]:
                    read_o = (n - 1, t)
                else:
                    read_o = None
                q0 = max(0, P * (j - TPC * c))
                for h in range(GH):
                    b = GH * t + h
                    act.wait_ge(s_score, b + 1)
                    if b >= 8:
                        act.wait_ge(s_pv, (b - 8) // GH + 1)
                    act.activation(wreg[:, b % 8, 0:CT - q0], bank(b % 3, CT - q0), ACT.Exp,
                                   scale=EXP_SCALE).then_inc(s_p, 1)
                if read_o is not None:
                    copy_o(act, *read_o)
            copy_o(act, NGRP - 1, len(steps))

            for i in range(TT):
                act.wait_ge(s_attT, i + 1)
                if i >= 2:
                    act.wait_ge(s_oproj, i - 1)
                act.activation(attT[:, i % 2, 0, :, :],
                               bank(2 + i % 2, D).rearrange("p (k t) -> p k t", k=KT), ACT.Copy).then_inc(s_atth, 1)

            x_high(2 * NCH)
            with act.Fori(0, NCH - 1) as c:
                ffn_chunk(c + NCH, c + (2 * NCH + 1))
            ffn_chunk(2 * NCH - 1, None)

        @block.vector
        def _(dve):
            step = [0]

            def own(ins):
                ins.then_inc(s_dve, 1)
                step[0] += 1
                dve.wait_ge(s_dve, step[0])

            dve.sem_inc(s_prod, 1)
            dve.sem_inc(s_resid, 1)

            dve.wait_ge(s_scales, 48)
            for k, s in enumerate((sg, su, sd)):
                dve.tensor_reduce(amax[:, k:k + 1], s[:, :, :].rearrange("p a b -> p (a b)"), AX.X, ALU.max,
                                  apply_absolute_value=True)
            dve.wait_ge(s_proj_in, 16)
            dve.tensor_reduce(amax[:, 3:4], proj_nat, AX.X, ALU.max,
                                  apply_absolute_value=True)
            dve.wait_ge(s_out_in, 16)
            dve.tensor_reduce(amax[:, 4:5], out_nat, AX.X, ALU.max,
                                  apply_absolute_value=True).then_inc(s_amax, 1)

            def statistics(chunk, n):
                dve.bn_stats(stats[:, n, :], xres[:, bass.ds(chunk * (TPC * D) + n * D, D)]).then_inc(s_dve, 1)

            def aggregate():
                for n in range(TPC):
                    last = dve.bn_aggr(mv[:, n, :], stats[:, n, :])
                last.then_inc(s_stats, 1)

            dve.wait_ge(s_x[0], 16)
            for n in range(TPC):
                statistics(0, n)
            step[0] += TPC
            dve.wait_ge(s_dve, step[0])
            aggregate()

            dve.wait_ge(s_amax_all, 1)
            own(dve.tensor_scalar(pow_r[:, :], amax_all[:, :], 2.0 ** -60, None, ALU.max))
            own(dve.tensor_scalar(pow_r[:, :].bitcast(i32), pow_r[:, :].bitcast(i32), 0x7F800000, None,
                                  ALU.bitwise_and))
            own(dve.tensor_scalar(pow_i[:, :].bitcast(i32), pow_r[:, :].bitcast(i32), -1.0, float(254 << 23),
                                  ALU.mult, ALU.add))
            dve.tensor_scalar(mul_w[:, 0:3], pow_i[:, 0:3], 2.0 ** (W_POW + FP4_POW), None, ALU.mult)
            dve.tensor_scalar(kappa[:, :], pow_i[:, 0:1], 2.0 ** (I_POW - X_POW - W_POW), None, ALU.mult)
            dve.tensor_scalar(gelu_in[:, :], pow_r[:, 0:1], 2.0 ** (-X_POW - W_POW), None, ALU.mult)
            dve.tensor_scalar(s_qk[:, :], pow_r[:, 3:4], 2.0 ** (-X_POW - P_POW), None, ALU.mult)
            dve.tensor_scalar(s_out[:, :], pow_r[:, 3:4], pow_r[:, 4:5], 2.0 ** (-V_POW - P_POW), ALU.mult, ALU.mult)
            own(dve.tensor_scalar(tmp1[:, :], pow_r[:, 0:1], pow_r[:, 1:2], 0.5 * 2.0 ** (-I_POW - W_POW),
                                  ALU.mult, ALU.mult))
            dve.tensor_scalar(s_down[:, :], tmp1[:, :], pow_r[:, 2:3], None, ALU.mult)
            own(dve.tensor_scalar(mul_w[:, 3:5], pow_i[:, 3:5], 2.0 ** P_POW, None, ALU.mult))
            for k, s in enumerate((sg, su, sd)):
                last = dve.tensor_scalar(s[:, :, :], s[:, :, :], mul_w[:, k:k + 1], None, ALU.mult)
            last.then_inc(s_scaled, 1)

            def weights_low(k):
                src, (high, low) = group_banks(k)
                dve.wait_ge(s_wh, k + 1)
                dve.tensor_tensor(low, src, high, ALU.subtract).then_inc(s_wl, 1)

            for n in range(3 * NPIECE):
                m, q = n // NPIECE, n % NPIECE
                if q == 0:
                    dve.wait_ge(s_packed[m], 16)
                nat = (gate_nat, up_nat, down_nat)[m]
                if m < 2:
                    w = nat[:, 512 * q:512 * q + 512]
                else:
                    w = nat.rearrange("p (k c) -> p k c", k=KT)[:, :, 256 * q:256 * q + 256]

                def like(t):
                    return t if m < 2 else t.rearrange("p (k c) -> p k c", k=KT)

                moved, spread, signs = bits[n % 2]
                if n >= 2:
                    dve.wait_ge(s_vals, n - 1)
                own(dve.tensor_scalar(like(moved), w, 0xF0, 12, ALU.bitwise_and, ALU.logical_shift_left))
                own(dve.scalar_tensor_tensor(out=like(spread), in0=w, scalar=0x0F, in1=like(moved),
                                             op0=ALU.bitwise_and, op1=ALU.bitwise_or))
                dve.tensor_scalar(moved, spread, 0x00070007, 9, ALU.bitwise_and, ALU.logical_shift_left)
                own(dve.tensor_scalar(signs, spread, 0x00080008, 12, ALU.bitwise_and, ALU.logical_shift_left))
                dve.tensor_tensor(code_pair[n % 2], moved, signs, ALU.bitwise_or).then_inc(s_code, 1)
                if n >= 2:
                    weights_low(2 * (n - 2))
                    weights_low(2 * (n - 2) + 1)
            dve.tensor_scalar(proj_nat, proj_nat, mul_w[:, 3:4], None, ALU.mult)
            dve.tensor_scalar(out_nat, out_nat, mul_w[:, 4:5], None, ALU.mult).then_inc(s_scaled, 1)
            for k in range(2 * (3 * NPIECE - 2), len(groups)):
                weights_low(k)

            def x_low(job):
                dve.wait_ge(s_xh, job + 1)
                dve.tensor_tensor(xT[:, 1, :, :], XT_BANKS, xT[:, 0, :, :], ALU.subtract).then_inc(s_xl, 1)

            FFN_STEPS = TPC

            def ffn_chunk(cc, c, job, chunk, base):
                def low(n):
                    dve.wait_ge(s_ihigh, cc * NT + (n + 1))
                    dve.tensor_tensor(inter[:, 1, n, :], prod_ring[:, n % 3, :], inter[:, 0, n, :],
                                      ALU.subtract).then_inc(s_inter, 1)

                dve.wait_ge(s_down_done, cc * TPC + 1)
                for n in range(NT):
                    if n >= 3:
                        dve.wait_ge(s_inter, cc * NT + (n - 2))
                    dve.wait_ge(s_up, cc * NT + (n + 1))
                    dve.wait_ge(s_gelu, cc * NT + (n + 2))
                    dve.scalar_tensor_tensor(out=prod_ring[:, n % 3, :], in0=bank(2 + n % 2),
                                             scalar=kappa[:, 0:1], in1=gelu_ring[:, n % 3, :],
                                             op0=ALU.mult, op1=ALU.mult).then_inc(s_prod, 1)
                    if job is not None and n == 4 + TPC:
                        dve.wait_ge(s_dve, base + TPC)
                    if n:
                        low(n - 1)
                    dve.wait_ge(s_prod, cc * NT + (n + 2))
                    dve.tensor_copy(inter[:, 0, n, :], prod_ring[:, n % 3, :]).then_inc(s_ihigh, 1)
                    if job is not None and 4 <= n < 4 + TPC:
                        if n == 4:
                            dve.wait_ge(s_yn, job)
                        statistics(chunk, n - 4)
                    if job is not None and n == 4 + TPC:
                        aggregate()
                low(NT - 1)
                if job is not None:
                    x_low(job)
                for n in range(TPC):
                    dve.wait_ge(s_down_done, cc * TPC + (n + 2))
                    dst = xres[:, bass.ds(c * (TPC * D) + n * D, D)]
                    dve.scalar_tensor_tensor(out=half_sum[:, n % 2, :], in0=down_bank(n)[:, D:2 * D],
                                             scalar=s_down[:, 0:1], in1=dst, op0=ALU.mult,
                                             op1=ALU.add).then_inc(s_half, 1)
                    dve.wait_ge(s_half, cc * TPC + (n + 1))
                    dve.scalar_tensor_tensor(out=dst, in0=down_bank(n)[:, 0:D], scalar=s_down[:, 0:1],
                                             in1=half_sum[:, n % 2, :], op0=ALU.mult,
                                             op1=ALU.add).then_inc(s_resid, 1)

            x_low(0)
            for k in range(1, NCH):
                dve.wait_ge(s_x[k], 16)
            with dve.Fori(0, NCH - 1) as c:
                ffn_chunk(c, c, c + 1, c + 1, c * FFN_STEPS + step[0])
            step[0] += FFN_STEPS * (NCH - 1)
            ffn_chunk(NCH - 1, NCH - 1, NCH, 0, step[0])
            step[0] += FFN_STEPS

            slot, read = [0], [0]

            def maxima(kind, n, unit):
                c, r = n // NG, n % 2
                at = 4 + 2 * (slot[0] % 2)
                if kind == "negate":
                    dve.wait_ge(s_aread, read[0])
                    m = m_part[:, r, 0, :]
                    if c >= 2:
                        own(dve.tensor_tensor(m, m, m_part[:, r, 1, :], ALU.max))
                    m = m.rearrange("p (a k) -> p a k", a=2)
                    own(dve.tensor_scalar(m_split[:, r, :, 0, :], m, -1.0 / MSCALE, None, ALU.mult))
                    dve.scalar_tensor_tensor(out=m_split[:, r, :, 1, :], in0=m, scalar=-1.0 / MSCALE,
                                             in1=m_split[:, r, :, 0, :], op0=ALU.mult,
                                             op1=ALU.subtract).then_inc(s_mneg, 1)
                    return
                dve.wait_ge(s_ascore, slot[0] + 1)
                if kind == "rows":
                    if n >= 2:
                        dve.wait_ge(s_mdma[r], 16 * 2 * (n // 2))
                    dve.tensor_copy(m_rows[:, r, :], ps[0:32, 512 * at:512 * at + P // 2].bitcast(f16))\
                       .then_inc(s_aread, 1)
                else:
                    segs, width, (part, q, h, cnt) = unit
                    if cnt == 2:
                        src = ps[:, 512 * at:512 * at + 1024].rearrange("p (a n) -> p a n", a=2)[:, :, 0:width]
                    else:
                        src = ps[:, 512 * at:512 * at + width].rearrange("p (a n) -> p a n", a=1)
                    col = 8 * (h % 2) + TPC * (h // 2) + q
                    dve.tensor_reduce(m_part[:, r, part, col:col + 8 * (cnt - 1) + 1:8], src, AX.X, ALU.max)\
                       .then_inc(s_aread, 1)
                    read[0] = slot[0] + 1
                slot[0] += 1

            for c in range(NCH):
                for m in range(4):
                    dve.wait_ge(s_qkh, 4 * c + m + 1)
                    dve.scalar_tensor_tensor(out=qk_flat[:, c % 2, 1, m, :], in0=bank(m % 2), scalar=s_qk[:, 0:1],
                                             in1=qk_flat[:, c % 2, 0, m, :], op0=ALU.mult,
                                             op1=ALU.subtract).then_inc(s_qkl, 1)
                    if c == NCH - 1:
                        for u in early_units(m):
                            maxima(*u)
                if c < NCH - 1:
                    dve.wait_ge(s_yn, NCH + c + 1)
                    for n in range(TPC):
                        statistics(c + 1, n)
                    step[0] += TPC
                    dve.wait_ge(s_dve, step[0])
                    aggregate()
                    x_low(NCH + c + 1)

            for k in range(4, QKV_GROUPS):
                for u in early_units(k):
                    maxima(*u)
            dve.wait_ge(s_v, TT)
            dve.memset(bank(3), 0.0).then_inc(s_o, 1)
            for t in range(len(steps)):
                for u in plan[t]:
                    maxima(*u)

            def o_normalised(i):
                dve.wait_ge(s_onat, i + 1)
                o = bank(i % 2).rearrange("p (h e) -> p h e", e=32)
                own(dve.reciprocal(recip[:, i % 2, :], o[:, :, HD]))
                a = att[:, i % 2, :].rearrange("p (h e) -> p h e", e=HD)
                dve.tensor_tensor(a, o[:, :, 0:HD],
                                  recip[:, i % 2, :].unsqueeze(2).to_broadcast([P, HEADS, HD]), ALU.mult)\
                   .then_inc(s_att, 1)

            def o_low(i):
                dve.wait_ge(s_atth, i + 1)
                dve.tensor_tensor(attT[:, i % 2, 1, :, :], bank(2 + i % 2, D).rearrange("p (k t) -> p k t", k=KT),
                                  attT[:, i % 2, 0, :, :], ALU.subtract).then_inc(s_attl, 1)

            def o_added(i):
                dve.wait_ge(s_oproj, i + 1)
                dst = xres[:, D * i:D * i + D]
                own(dve.scalar_tensor_tensor(out=half_sum[:, i % 2, :], in0=down_bank(i)[:, D:2 * D],
                                             scalar=s_out[:, 0:1], in1=dst, op0=ALU.mult, op1=ALU.add))
                dve.scalar_tensor_tensor(out=dst, in0=down_bank(i)[:, 0:D], scalar=s_out[:, 0:1],
                                         in1=half_sum[:, i % 2, :], op0=ALU.mult,
                                         op1=ALU.add).then_inc(s_oresid, 1)

            for i in range(TT + 2):
                if i < TT:
                    o_normalised(i)
                if 1 <= i <= TT:
                    o_low(i - 1)
                if i >= 2:
                    o_added(i - 2)
                if i == TPC + 2:
                    dve.wait_ge(s_oresid, TPC)
                    for n in range(TPC):
                        statistics(0, n)
                    step[0] += TPC
                    dve.wait_ge(s_dve, step[0])
                    aggregate()
            x_low(2 * NCH)
            dve.wait_ge(s_oresid, TT)
            with dve.Fori(0, NCH - 1) as c:
                ffn_chunk(c + NCH, c, c + (2 * NCH + 1), c + 1, c * FFN_STEPS + step[0])
            ffn_chunk(2 * NCH - 1, NCH - 1, None, None, None)

        @block.tensor
        def _(pe):
            pe.sem_inc(s_down_done, 1)
            pe.wait_ge(s_const, 1)

            for k, (kind, j) in enumerate(groups):
                dst = bank(k % W_BANKS)
                if kind in ("gate", "up", "down"):
                    n = k // 2
                    pe.wait_ge(s_vals, n + 1)
                else:
                    pe.wait_ge(s_scaled, 2)
                if k >= W_BANKS:
                    pe.wait_ge(s_wl, k - W_BANKS + 1)
                for a in range(2):
                    for kt in range(KT):
                        if kind in ("gate", "up"):
                            v = vals[n % 4].rearrange("p (r k j) -> p r k j", r=4, k=2)
                            src, at = v[:, 2 * (j % 2) + a, kt, :], D * kt + P * a
                        elif kind == "down":
                            v = vals[n % 4].rearrange("p (r k j) -> p r k j", r=2, k=2)
                            src, at = v[:, a, kt, P * (j % 2):P * (j % 2) + P], D * kt + P * a
                        elif kind == "proj":
                            v = proj_nat.rearrange("p (m j k) -> p m j k", m=6, k=2)
                            src, at = v[:, 2 * j + a, :, kt], D * kt + P * a
                        else:
                            v = out_nat.rearrange("p (m k j) -> p m k j", m=2, k=2)
                            src, at = v[:, a, kt, :], D * kt + P * a
                        last = pe.transpose(dst[:, at:at + P], src, ident[:, :])
                last.then_inc(s_wt, 1)

            def transpose_x(job):
                pe.wait_ge(s_yn, job + 1)
                for n in range(TPC):
                    v = yn[:, n, :].rearrange("p (j k) -> p j k", k=KT)
                    for kt in range(KT):
                        last = pe.transpose(XT_BANKS[:, kt, P * n:P * n + P], v[:, :, kt], ident[:, :])
                last.then_inc(s_xt, 1)

            def three_passes(dst, w, cols):
                for kt in range(KT):
                    pe.matmul(dst, w[:, 0, kt, cols], xT[:, 0, kt, :], start=(kt == 0), stop=False)
                    pe.matmul(dst, w[:, 0, kt, cols], xT[:, 1, kt, :], start=False, stop=False)
                    last = pe.matmul(dst, w[:, 1, kt, cols], xT[:, 0, kt, :], start=False, stop=(kt == KT - 1))
                return last

            def ffn_chunk(cc, job_here, job):
                pe.wait_ge(s_xl, job_here + 1)
                for n in range(NT):
                    cols = slice(P * n, P * n + P)
                    pe.wait_ge(s_gelu, cc * NT + (1 if n < 2 else n))
                    three_passes(bank(n % 2), wg, cols).then_inc(s_gate, 1)
                    pe.wait_ge(s_prod, cc * NT + (1 if n < 2 else n))
                    three_passes(bank(2 + n % 2), wu, cols).then_inc(s_up, 1)
                if job is not None:
                    transpose_x(job)
                for m in range(TPC):
                    pe.wait_ge(s_resid, cc * TPC + (1 if m < 2 else m))
                    tok = slice(P * m, P * m + P)
                    for n in range(NT):
                        if m == 0:
                            pe.wait_ge(s_inter, cc * NT + (n + 1))
                        pe.matmul(down_bank(m), inter[:, 0, n, tok], wd[:, n, :], start=(n == 0), stop=False)
                        last = pe.matmul(down_bank(m)[:, 0:D], inter[:, 1, n, tok], wd[:, n, 0:D],
                                         start=False, stop=(n == NT - 1))
                    last.then_inc(s_down_done, 1)

            transpose_x(0)
            with pe.Fori(0, NCH - 1) as c:
                ffn_chunk(c, c, c + 1)
            ffn_chunk(NCH - 1, NCH - 1, NCH)

            slot = [0]

            def maximum_unit(kind, n, unit):
                if kind == "negate":
                    return
                c, g = n // NG, n % NG
                at = 4 + 2 * (slot[0] % 2)
                if slot[0] >= 2:
                    pe.wait_ge(s_aread, slot[0] - 1)
                if kind == "rows":
                    pe.wait_ge(s_mneg, n + 1)
                    last = pe.transpose(ps[0:32, 512 * at:512 * at + P // 2].bitcast(f16),
                                        m_split[:, n % 2, :, :, :].rearrange("p a s k -> p (a s k)"), ident16[:, :])
                else:
                    if g == 0 and c and unit[2][1:3] == (0, 0) and unit[2][0] == 0:
                        pe.wait_ge(s_stack[c], 16 * 12)
                    for k, (h, i, k0, k1) in enumerate(unit[0]):
                        half, pair = 64 * (h % 2), 2 * g + h // 2
                        for m in range(k0, k1, 512):
                            w = min(512, k1 - m)
                            dst = bank(at + k + (m - k0) // 512, w)
                            diag = P * i - m
                            last = pe.matmul(dst, qreg[half:half + 3 * HD, c, pair, P * (i - TPC * c):P * (i - TPC * c) + P],
                                             kreg[half:half + 3 * HD, pair, m:m + w],
                                             start=True, stop=not 0 <= diag < w)
                            if 0 <= diag < w:
                                last = masked(dst[:, diag:diag + P], tri_a, half)
                last.then_inc(s_ascore, 1)
                slot[0] += 1

            def masked(dst, tri, half):
                for r in range(2):
                    last = pe.matmul(dst[:, 64 * r:64 * r + 64], tri[half:half + 64, r, :],
                                     big_id[half:half + 64, :], start=False, stop=(r == 1))
                return last

            def scores(t, h):
                n, c, g, j = steps[t]
                b = GH * t + h
                if b >= 3:
                    pe.wait_ge(s_p, b - 2)
                half, pair = 64 * (h % 2), 2 * g + h // 2
                q0 = max(0, P * (j - TPC * c))
                dst = bank(b % 3, CT - q0)
                diag = j >= TPC * c
                rows = slice(half, half + 3 * HD + 2)
                last = pe.matmul(dst, kreg[rows, pair, P * j:P * j + P], qreg[rows, c, pair, q0:CT],
                                 start=True, stop=not diag)
                if diag:
                    last = masked(dst[:, 0:P], tri_b, half)
                last.then_inc(s_score, 1)

            def weighted_values(t):
                n, c, g, j = steps[t]
                q0 = max(0, P * (j - TPC * c))
                if j == 0:
                    pe.wait_ge(s_o, n + 1)
                for h in range(GH):
                    b = GH * t + h
                    pe.wait_ge(s_p, b + 1)
                    last = pe.matmul(bank(3, CT - q0, q0)[32 * h:32 * h + HD + 1, :], v1[:, j, GH * g + h, :],
                                     wreg[:, b % 8, 0:CT - q0], start=(j == 0), stop=(j == TPC * (c + 1) - 1))
                last.then_inc(s_pv, 1)

            for c in range(NCH):
                pe.wait_ge(s_xl, NCH + c + 1)
                if c == NCH - 1:
                    pe.wait_ge(s_const, 2)
                    pe.wait_ge(s_resid, 1 + TPC * NCH)
                for m in range(4):
                    if 4 * c + m >= 2:
                        pe.wait_ge(s_qkl, 4 * c + m - 1)
                    three_passes(bank(m % 2), wp, slice(P * m, P * m + P)).then_inc(s_qk_ps, 1)
                    if c == NCH - 1:
                        if m == 0:
                            pe.wait_ge(s_stack[0], 16 * 12)
                        for u in early_units(m):
                            maximum_unit(*u)
                for n in range(TPC):
                    if TPC * c + n >= 2:
                        pe.wait_ge(s_v, TPC * c + n - 1)
                    dst, tok = bank(2 + n % 2, D), slice(P * n, P * n + P)
                    for kt in range(KT):
                        cols = slice(2 * D, 3 * D)
                        pe.matmul(dst, xT[:, 0, kt, tok], wp[:, 0, kt, cols], start=(kt == 0), stop=False)
                        pe.matmul(dst, xT[:, 0, kt, tok], wp[:, 1, kt, cols], start=False, stop=False)
                        last = pe.matmul(dst, xT[:, 1, kt, tok], wp[:, 0, kt, cols], start=False,
                                         stop=(kt == KT - 1))
                    last.then_inc(s_v_ps, 1)
                    if c == NCH - 1:
                        for u in early_units(4 + n):
                            maximum_unit(*u)
                if c < NCH - 1:
                    transpose_x(NCH + c + 1)

            pe.wait_ge(s_qkl, 4 * NCH)
            pe.wait_ge(s_v, TT)
            for t in range(len(steps)):
                if t == first_step[steps[t][0]]:
                    n = steps[t][0]
                    pe.wait_ge(s_mdma[n % 2], 16 * 2 * (n // 2 + 1))
                units = plan[t]
                scores(t, 0)
                scores(t, 1)
                for u in units[:len(units) // 2]:
                    maximum_unit(*u)
                scores(t, 2)
                scores(t, 3)
                for u in units[len(units) // 2:]:
                    maximum_unit(*u)
                if t:
                    weighted_values(t - 1)
            weighted_values(len(steps) - 1)

            for i in range(TT + 2):
                if i < TT:
                    c, q = i // TPC, i % TPC
                    if i == 0:
                        pe.wait_ge(s_p, GH * len(steps))
                        pe.wait_ge(s_o, 1 + NGRP)
                    if i >= 2:
                        pe.wait_ge(s_att, i - 1)
                    for g in range(NG):
                        last = pe.transpose(bank(i % 2, P, P * g),
                                            oT[:, c, g, P * q:P * q + P], ident[:, :])
                    last.then_inc(s_onat, 1)
                if 1 <= i <= TT:
                    k = i - 1
                    pe.wait_ge(s_att, k + 1)
                    if k >= 2:
                        pe.wait_ge(s_attl, k - 1)
                    for kt in range(KT):
                        last = pe.transpose(bank(2 + k % 2, P, P * kt), att[:, k % 2, P * kt:P * kt + P], ident[:, :])
                    last.then_inc(s_attT, 1)
                if i >= 2:
                    k = i - 2
                    pe.wait_ge(s_attl, k + 1)
                    if k >= 2:
                        pe.wait_ge(s_oresid, k - 1)
                    for kt in range(KT):
                        pe.matmul(down_bank(k), attT[:, k % 2, 0, kt, :], wo[:, kt, :], start=(kt == 0), stop=False)
                        last = pe.matmul(down_bank(k)[:, 0:D], attT[:, k % 2, 1, kt, :], wo[:, kt, 0:D],
                                         start=False, stop=(kt == KT - 1))
                    last.then_inc(s_oproj, 1)

            transpose_x(2 * NCH)
            pe.wait_ge(s_oresid, TT)
            with pe.Fori(0, NCH - 1) as c:
                ffn_chunk(c + NCH, c + 2 * NCH, c + (2 * NCH + 1))
            ffn_chunk(2 * NCH - 1, 3 * NCH - 1, None)


_INS = ["L0_attn_x", "L0_attn_w_project", "L0_attn_w_out", "L0_ffn_gate_W_packed", "L0_ffn_gate_scales",
        "L0_ffn_up_W_packed", "L0_ffn_up_scales", "L0_ffn_down_W_packed", "L0_ffn_down_scales"]


def kernel(**inputs):
    import numpy as _np
    import concourse.bacc as _bacc
    from concourse import mybir as _mybir
    from concourse.bass_utils import run_bass_kernel_spmd as _run

    nc = _bacc.Bacc("TRN2", target_bir_lowering=False, num_devices=1)
    arrays, args = {}, []
    for name in _INS:
        a = _np.ascontiguousarray(inputs[name])
        arrays[f"in_{name}"] = a
        args.append(nc.dram_tensor(f"in_{name}", a.shape, _mybir.dt.from_np(a.dtype), kind="ExternalInput").ap())
    shape = inputs["L0_attn_x"].shape
    args.append(nc.dram_tensor("out_x", shape, _mybir.dt.float32, kind="ExternalOutput").ap())
    macaron_block(nc, *args)
    r = _run(nc, [arrays], core_ids=[0])
    return r.results[0]["out_x"]
```

```python
import concourse.bass as bass
from concourse import mybir
from contextlib import ExitStack


def macaron_block(nc, x, w_project, w_out, gate_packed, gate_scales, up_packed, up_scales,
                  down_packed, down_scales, out):
    f32, f16, i32 = mybir.dt.float32, mybir.dt.float16, mybir.dt.int32
    ALU, ACT, AX = mybir.AluOpType, mybir.ActivationFunctionType, mybir.AxisListType

    P = 128
    T, D = x.shape[1], x.shape[2]
    F = gate_packed.shape[0]
    BLK = D // gate_scales.shape[1]
    HEADS, HD = 16, D // 16
    TT = T // P
    CT = 512
    NCH = T // CT
    TPC = CT // P
    NT = F // P
    KT = D // P
    NJ = NT // 2
    EPS = 1e-5
    GH = 4
    NG = HEADS // GH
    NPAIR = HEADS // 2
    BIG = 30000.0
    MSCALE = 256.0
    MSCALE_PAIR = 0x5C005C00
    EXP_SCALE = float(HD) ** -0.5

    X_POW, W_POW, P_POW, V_POW = 11, 12, 14, 6
    I_POW = -8
    FP4_POW = 14

    ctx = ExitStack()
    with ctx:
        def sb(name, shape, dt):
            return ctx.enter_context(nc.sbuf_tensor(name, shape, dt))

        def sem(name):
            return ctx.enter_context(nc.semaphore(name))

        xres = sb("xres", [P, TT * D], f32)
        yn = sb("yn", [P, TPC, D], f32)
        xT = sb("xT", [P, 2, 2, KT, CT], f16)
        wg = sb("wg", [P, 2, KT, F], f16)
        wu = sb("wu", [P, 2, KT, F], f16)
        wd = sb("wd", [P, NT, 2 * D], f16)
        wp = sb("wp", [P, 2, KT, 3 * D], f16)
        wo = sb("wo", [P, KT, 2 * D], f16)
        v1 = sb("v1", [P, TT, HEADS, HD + 1], f32)
        ident = sb("ident", [P, P], f32)
        big_id = sb("big_id", [P, P], f16)
        tri_a = sb("tri_a", [P, P], f16)
        tri_b = sb("tri_b", [P, P], f16)
        zero_rows = sb("zero_rows", [2, P], f16)
        sg = sb("sg", [P, NT, D // BLK], f32)
        su = sb("su", [P, NT, D // BLK], f32)
        sd = sb("sd", [P, KT, F // BLK], f32)
        amax = sb("amax", [P, 5], f32)
        amax_all = sb("amax_all", [P, 5], f32)
        pow_r = sb("pow_r", [P, 5], f32)
        pow_i = sb("pow_i", [P, 5], f32)
        mul_w = sb("mul_w", [P, 5], f32)
        gelu_in = sb("gelu_in", [P, 1], f32)
        kappa = sb("kappa", [P, 1], f32)
        s_down = sb("s_down", [P, 1], f32)
        s_qk = sb("s_qk", [P, 1], f32)
        s_out = sb("s_out", [P, 1], f32)
        tmp1 = sb("tmp1", [P, 1], f32)
        stats = sb("stats", [P, TPC, 6], f32)
        mv = sb("mv", [P, TPC, 2], f32)
        neg_mean = sb("neg_mean", [P, TPC], f32)
        rstd = sb("rstd", [P, TPC], f32)
        minus_half = sb("minus_half", [P, TPC], f32)
        half_sum = sb("half_sum", [P, 2, D], f32)
        m_part = sb("m_part", [P, 2, 2, 16], f32)
        m_split = sb("m_split", [P, 2, 2, 2, 8], f16)
        m_rows = sb("m_rows", [32, 2, P], f16)
        ident16 = sb("ident16", [P, P], f16)
        att = sb("att", [P, 2, D], f32)
        attT = sb("attT", [P, 2, 2, KT, P], f16)
        recip = sb("recip", [P, 2, HEADS], f32)
        oT = sb("oT", [P, NG, CT], f32)

        qreg = sb("qreg", [P, 2, 2, NPAIR, CT], f16)
        kreg = sb("kreg", [P, NPAIR, T], f16)
        wreg = sb("wreg", [P, 8, CT], f32)
        qflat = qreg[:, :, :, :, :].rearrange("p c h a t -> p (c h a t)")
        inter = qflat.rearrange("p (s n t) -> p s n t", s=2, n=NT)
        kflat = kreg[:, :, :].rearrange("p a t -> p (a t)").bitcast(i32)
        gate_nat, up_nat, down_nat = (kflat[:, k * 2048:(k + 1) * 2048] for k in range(3))
        proj_nat = kflat[:, 6144:6144 + 1536].bitcast(f32)
        out_nat = kflat[:, 7680:8192].bitcast(f32)
        code_pair = [[oT[:, 2 * k + m, :].bitcast(i32) for m in range(2)] for k in range(2)]
        v_flat = v1[:, :, :, :].rearrange("p a h e -> p (a h e)")
        vals = [v_flat[:, 1024 * k:1024 * (k + 1)] for k in range(4)]
        gelu_ring = wreg[:, 0:3, :]
        prod_ring = wreg[:, 3:6, :]
        qk_flat = wreg[:, :, :].bitcast(f16).rearrange("p a b -> p (a b)")\
            .rearrange("p (r s m t) -> p r s m t", r=2, s=2, m=4)

        qk_dram = nc.dram_tensor("qk_split", [2, 4, P, T], f16, kind="Internal").ap()
        ps = ctx.enter_context(nc.psum_tensor("ps", [P, 8 * 512], f32))

        def bank(b, n=512, at=0):
            return ps[:, 512 * b + at:512 * b + at + n]

        s_scales, s_packed = sem("scales_in"), [sem(f"packed_in{k}") for k in range(3)]
        s_proj_in, s_out_in = sem("proj_in"), sem("w_out_in")
        s_x = [sem(f"x_in{k}") for k in range(NCH)]
        s_const = sem("constants")
        s_pool = sem("pool_step")
        s_dve = sem("dve_step")
        s_amax, s_amax_all = sem("amax"), sem("amax_all")
        s_scaled = sem("scales_scaled")
        s_code = sem("codes_decoded")
        s_vals = sem("weights_decoded")
        s_wt = sem("weights_transposed")
        s_wh, s_wl = sem("weights_high"), sem("weights_low")
        s_stats, s_yn = sem("stats_ready"), sem("normalised")
        s_xt, s_xh, s_xl = sem("x_transposed"), sem("xT_high"), sem("xT_low")
        s_gate, s_up = sem("gate_products"), sem("up_products")
        s_gelu, s_prod = sem("gelu_done"), sem("product_done")
        s_ihigh, s_inter = sem("inter_high"), sem("inter_ready")
        s_down_done, s_half, s_resid = sem("down_products"), sem("residual_half"), sem("residual_done")
        s_qk_ps, s_v_ps = sem("qk_products"), sem("v_products")
        s_qkh, s_qkl, s_v = sem("qk_high"), sem("qk_low"), sem("v_ready")
        s_qk_out, s_ones = sem("qk_in_dram"), sem("key_ones")
        s_kstack = [sem(f"key_stacks_in{k}") for k in range(NCH)]
        s_qstack = [sem(f"query_stacks_in{k}") for k in range(NCH)]
        s_qzero = sem("query_stacks_zeroed")
        s_slot, s_slot_read = sem("slot_written"), sem("slot_read")
        s_mneg = sem("maxima_ready")
        s_mdma = [sem("max_rows_in0"), sem("max_rows_in1")]
        s_score, s_p, s_pv, s_o = sem("scores"), sem("probs"), sem("pv_done"), sem("o_read")
        s_store = sem("stored")

        block = ctx.enter_context(nc.Block())

        NPIECE = 4
        pieces = [(m, q) for q in range(NPIECE) for m in range(2)] + [(2, q) for q in range(NPIECE)]
        groups = [(("gate", "up", "down")[m], 2 * q + a) for m, q in pieces for a in range(2)] + \
                 [("proj", j) for j in range(3)] + [("out", 0)]
        W_BANKS = 2
        FIRST_PIECES = 2
        behind = [[] for _ in range(NT)]
        for p, n in zip(range(FIRST_PIECES, 3 * NPIECE), (0, 1, 3, 4, 6, 8, 9, 10, 11, 12)):
            behind[n] += [2 * p, 2 * p + 1]
        behind[13] += [6 * NPIECE, 6 * NPIECE + 1]
        behind[14] += [6 * NPIECE + 2, 6 * NPIECE + 3]
        POWER_TILE, PROJ_TILE = 3, 6
        DECODE_AHEAD = 4

        LEAD = 1700
        steps = [(NG * c + g, c, g, j) for c in range(NCH) for g in range(NG) for j in range(TPC * (c + 1))]
        first_step = {}
        for t, (n, _, _, _) in enumerate(steps):
            first_step.setdefault(n, t)
        NGRP = NG * NCH

        def max_units(c, g):
            units = []
            for q in range(TPC):
                i = TPC * c + q
                n = P * (i + 1)
                if n <= 512:
                    for h in (0, 2):
                        units.append(([(h, i, 0, n), (h + 1, i, 0, n)], n, (0, q, h, 2)))
                else:
                    for h in range(GH):
                        units.append(([(h, i, 0, min(n, 1024))], min(n, 1024), (0, q, h, 1)))
                    if n > 1536:
                        for h in range(GH):
                            units.append(([(h, i, 1024, n)], n - 1024, (1, q, h, 1)))
                    elif n > 1024:
                        for h in (0, 2):
                            units.append(([(h, i, 1024, n), (h + 1, i, 1024, n)], n - 1024, (1, q, h, 2)))
            return units

        def columns(unit):
            return sum(k1 - k0 for _, _, k0, k1 in unit[2][0]) + 128

        def step_columns(t):
            _, c, _, j = steps[max(t, 0)]
            return min(CT, P * (TPC * (c + 1) - j)) + 128

        plan = {t: [] for t in range(-1, len(steps) + 1)}
        for n in range(NGRP):
            c, g = n // NG, n % NG
            units = [("unit", n, u) for u in max_units(c, g)]
            start, end = (end if n else 0), first_step[n]
            while sum(step_columns(k) for k in range(end, first_step[n])) < LEAD:
                end -= 1
            todo, done, t = sum(columns(u) for u in units), 0, start
            room = [step_columns(k) for k in range(start, end)]
            for u in units:
                while n and t < end - 1 and sum(room[:t + 1 - start]) * todo <= done * sum(room):
                    t += 1
                plan[max(t, -1) if n else -1].append(u)
                done += columns(u)
            plan[max(end - 1, -1)].append(("negate", n, None))
            plan[max(end, 0) if n else -1].append(("rows", n, None))
        first = plan[-1].index(("negate", 0, None))
        own_units, later = plan[-1][:first], [u for u in plan[-1][first + 1:] if u != ("rows", 0, None)]
        early = [own_units[2 * m:2 * m + 2] for m in range(4)]
        early[3].append(("negate", 0, None))
        early += [[("rows", 0, None)]] + [[] for _ in range(TPC - 1)]
        for k, u in enumerate(later):
            early[4 + TPC * k // len(later)].append(u)
        plan[-1] = [u for stage in early for u in stage]

        for c in range(NCH):
            for q in range(TPC):
                i = TPC * c + q
                for stage, kind in enumerate(("o", "split", "project")):
                    if c < NCH - 1:
                        plan[first_step[NG * (c + 1)] + 2 + q + stage].append((kind, i, None))
        for k in range(TPC + 2):
            for stage, kind in ((2, "project"), (1, "split"), (0, "o")):
                if 0 <= k - stage < TPC:
                    plan[len(steps)].append((kind, TPC * (NCH - 1) + k - stage, None))
        LN_STEP = first_step[NG + 1] + 1
        plan[LN_STEP].append(("statistics", 2 * NCH, None))
        plan[LN_STEP + 3].append(("transpose", 2 * NCH, None))

        in_slots = [(kind, n) for t in sorted(plan) for kind, n, _ in plan[t] if kind not in ("negate", "statistics")]
        place = {item: k + 1 for k, item in enumerate(in_slots) if item[0] != "unit"}

        score_bank, last_in_bank, user = [], [], {}
        for b in range(GH * len(steps)):
            k = b - GH * first_step[NGRP - 1]
            score_bank.append(b % 3 if k < 0 else (0, 1, 2, 4, 5, 6, 7)[k % 7])
            last_in_bank.append(user.get(score_bank[b]))
            user[score_bank[b]] = b

        @block.sync
        def _(sp):
            sp.dma_start(sg[:, :, :].rearrange("p (j two) b -> p j (two b)", two=2),
                         gate_scales.rearrange("(j p two) b -> p j (two b)", p=P, two=2)).then_inc(s_scales, 16)
            sp.dma_start(su[:, :, :].rearrange("p (j two) b -> p j (two b)", two=2),
                         up_scales.rearrange("(j p two) b -> p j (two b)", p=P, two=2)).then_inc(s_scales, 16)
            sp.dma_start(sd[:, :, :], down_scales.rearrange("(k p) b -> p k b", p=P)).then_inc(s_scales, 16)
            for k, (dst, src) in enumerate(((gate_nat, gate_packed), (up_nat, up_packed))):
                sp.dma_start(dst.rearrange("p (j r) -> p j r", j=NJ),
                             src.rearrange("(j p two) c -> p j (two c)", p=P, two=2)).then_inc(s_packed[k], 16)
            sp.dma_start(down_nat.rearrange("p (k c) -> p k c", k=KT),
                         down_packed.rearrange("(k p) c -> p k c", p=P)).then_inc(s_packed[2], 16)
            sp.dma_start(proj_nat.rearrange("p (m d) -> p m d", d=D),
                         w_project.rearrange("(m p) d -> p m d", p=P)).then_inc(s_proj_in, 16)
            sp.dma_start(out_nat.rearrange("p (m d) -> p m d", d=D),
                         w_out.rearrange("(m p) d -> p m d", p=P)).then_inc(s_out_in, 16)

            def stack_source(c, m0, half, part):
                return qk_dram[part, m0:m0 + 2, :, CT * c:CT * (c + 1)]\
                    .rearrange("m (p a d) t -> a d (m p) t", a=2, d=HD)[half]

            def load_keys(c, which):
                for k in which:
                    half, row = k // 3, k % 3
                    r = 64 * half + HD * row
                    sp.dma_start(kreg[r:r + HD, :, CT * c:CT * (c + 1)],
                                 stack_source(c, 2, half, (0, 0, 1)[row])).then_inc(s_kstack[c], 16)

            def load_queries(c):
                if c >= 2:
                    sp.wait_ge(s_score, GH * first_step[NG * (c - 1)])
                for half in range(2):
                    for row in range(3):
                        r = 64 * half + HD * row
                        sp.dma_start(qreg[r:r + HD, c % 2, half, :, :],
                                     stack_source(c, 0, half, (0, 1, 0)[row])).then_inc(s_qstack[c], 16)
                    if c >= 2:
                        r = 64 * half + 3 * HD
                        sp.dma_start(qreg[r:r + 2, c % 2, half, :, :].rearrange("r a (q t) -> r (a q) t", t=P),
                                     zero_rows[:, :].unsqueeze(1).to_broadcast([2, NPAIR * TPC, P]))\
                          .then_inc(s_qstack[c], 16)

            sp.wait_ge(s_ones, 1)
            for c in range(NCH):
                cols = slice(CT * c, CT * (c + 1))
                sp.wait_ge(s_qkl, 4 * c + 4)
                sp.dma_start(qk_dram[:, :, :, cols].rearrange("s m p t -> p s m t"),
                             qk_flat[:, c % 2, :, :, :]).then_inc(s_qk_out, 16)
                sp.wait_ge(s_qk_out, 16 * (c + 1))
                if c < NCH - 1:
                    load_keys(c, range(6))
                if c == 0:
                    sp.wait_ge(s_qzero, 1)
                if c < 2:
                    load_queries(c)

            for n in range(NGRP):
                c, g = n // NG, n % NG
                sp.wait_ge(s_slot_read, place['rows', n])
                for a in range(2):
                    r = 64 * a + 3 * HD
                    dst = qreg[r:r + 2, c % 2, a, 2 * g:2 * g + 2, :].rearrange("r a t -> r (a t)")
                    sp.dma_start(dst.rearrange("r (k q) -> r k q", q=P),
                                 m_rows[16 * a:16 * a + 16, n % 2, :]).then_inc(s_mdma[n % 2], 16)
                if n < 3:
                    load_keys(NCH - 1, (2 * n, 2 * n + 1))
                if n % NG == 1 and 0 < n // NG < NCH - 1:
                    load_queries(n // NG + 1)

            for c in range(NCH):
                sp.wait_ge(s_resid, 1 + TPC * (NCH + c + 1))
                sp.dma_start(out[0, CT * c:CT * (c + 1), :].rearrange("(n p) d -> p n d", p=P),
                             xres[:, TPC * D * c:TPC * D * (c + 1)].rearrange("p (n d) -> p n d", d=D))\
                  .then_inc(s_store, 16)
            sp.wait_ge(s_store, 16 * NCH)

        def normalise(pool, own, job, chunk):
            pool.wait_ge(s_stats, job + 1)
            own(pool.tensor_scalar(neg_mean[:, :], mv[:, :, 0], -1.0, None, ALU.mult))
            own(pool.tensor_scalar(rstd[:, :], mv[:, :, 1], EPS, 2.0 ** (-2 * X_POW), ALU.add, ALU.mult))
            own(pool.tensor_tensor(rstd[:, :], rstd[:, :], minus_half[:, :], ALU.pow))
            if job:
                pool.wait_ge(s_xt, job)
            for n in range(TPC):
                last = pool.tensor_scalar(yn[:, n, :], xres[:, D * (TPC * chunk + n):D * (TPC * chunk + n + 1)],
                                          neg_mean[:, n:n + 1], rstd[:, n:n + 1], ALU.add, ALU.mult)
            last.then_inc(s_yn, 1)

        @block.gpsimd
        def _(pool):
            step = [0]

            def own(ins):
                ins.then_inc(s_pool, 1)
                step[0] += 1
                pool.wait_ge(s_pool, step[0])

            own(pool.memset(ident[:, :], 0.0))
            pool.affine_select(out=ident[:, :], in_=ident[:, :], compare_op=ALU.not_equal, fill=1.0,
                               base=0, pattern=[[-1, P]], channel_multiplier=1).then_inc(s_const, 1)
            own(pool.memset(minus_half[:, :], -0.5))
            own(pool.memset(ident16[:, :], 0.0))
            own(pool.affine_select(out=ident16[:, :], in_=ident16[:, :], compare_op=ALU.not_equal, fill=1.0,
                                   base=0, pattern=[[-1, P]], channel_multiplier=1))

            def all_reduce(k, cols):
                pool.wait_ge(s_amax, k)
                pool.partition_all_reduce(amax_all[:, cols], amax[:, cols], P, bass.bass_isa.ReduceOp.max)\
                    .then_inc(s_amax_all, 1)

            all_reduce(1, slice(0, 3))

            pool.wait_ge(s_scaled, 1)
            def decoded(n):
                m, q = pieces[n]
                pool.wait_ge(s_code, n + 1)
                if n >= 4:
                    pool.wait_ge(s_wt, 2 * (n - 4) + 2)
                rows = 4 if m < 2 else KT
                codes = [c.bitcast(f16).rearrange("p (r j two) -> p r j two", r=rows, two=2)[:, :, :, 1]
                         for c in code_pair[n % 2]]
                scales = (sg[:, 4 * q:4 * q + 4, :], su[:, 4 * q:4 * q + 4, :], sd[:, :, 16 * q:16 * q + 16])[m]
                for k in range(2):
                    dst = vals[n % 4].rearrange("p (r k j) -> p r k j", r=rows, k=2)[:, :, k, :]\
                        .rearrange("p r (b e) -> p r b e", e=BLK // 2)
                    last = pool.tensor_tensor(
                        dst, codes[k].rearrange("p r (b e) -> p r b e", e=BLK // 2),
                        scales.unsqueeze(3).to_broadcast(list(dst.shape)), ALU.mult)
                last.then_inc(s_vals, 1)

            for n in range(6):
                decoded(n)
                if n == 1:
                    normalise(pool, own, 0, 0)
            for n in range(NT):
                pool.wait_ge(s_ihigh, n + 1)
                pool.tensor_tensor(inter[:, 1, n, :], prod_ring[:, n % 3, :], inter[:, 0, n, :],
                                   ALU.subtract).then_inc(s_inter, 1)
                if behind[n] and behind[n][0] // 2 + DECODE_AHEAD < 3 * NPIECE:
                    decoded(behind[n][0] // 2 + DECODE_AHEAD)
                if n == POWER_TILE - 1:
                    all_reduce(2, slice(3, 5))
                if n == PROJ_TILE:
                    pool.wait_ge(s_scaled, 2)
                    pool.tensor_scalar(proj_nat, proj_nat, mul_w[:, 3:4], None, ALU.mult)
                    pool.tensor_scalar(out_nat, out_nat, mul_w[:, 4:5], None, ALU.mult).then_inc(s_scaled, 1)
                if n == 12:
                    normalise(pool, own, 1, 1)

            pool.memset(tri_a[:, :], -BIG)
            pool.memset(tri_b[:, :], -BIG)
            pool.memset(zero_rows[:, :], 0.0)
            own(pool.memset(big_id[:, :], 0.0))
            pool.affine_select(out=big_id[:, :], in_=big_id[:, :], compare_op=ALU.not_equal, fill=BIG,
                               base=0, pattern=[[-1, P]], channel_multiplier=1)
            pool.affine_select(out=tri_a[:, :], in_=tri_a[:, :], compare_op=ALU.is_gt, fill=0.0,
                               base=0, pattern=[[-1, P]], channel_multiplier=1)
            last = pool.affine_select(out=tri_b[:, :], in_=tri_b[:, :], compare_op=ALU.is_gt, fill=0.0,
                                      base=0, pattern=[[1, P]], channel_multiplier=-1)
            last.then_inc(s_const, 1)
            pool.wait_ge(s_const, 2)

            pool.wait_ge(s_wt, len(groups))
            pool.memset(v1[:, :, :, :], 1.0)
            pool.memset(kflat, MSCALE_PAIR).then_inc(s_ones, 1)
            pool.wait_ge(s_ones, 1)

            for job in range(2, 3 * NCH):
                normalise(pool, own, job, job % NCH)
                if job == NCH + 1:
                    pool.wait_ge(s_down_done, 1 + TPC * NCH)
                    pool.memset(qflat.bitcast(i32), 0).then_inc(s_qzero, 1)
                    pool.wait_ge(s_qzero, 1)

        def w_bank(k):
            return bank(4 + k % W_BANKS)

        def group_banks(k):
            kind, j = groups[k]
            src = w_bank(k).rearrange("p (k n) -> p k n", k=KT)
            if kind in ("gate", "up", "proj"):
                w = {"gate": wg, "up": wu, "proj": wp}[kind]
                return src, [w[:, s, :, 256 * j:256 * j + 256] for s in range(2)]
            w, a = (wd, 2 * j) if kind == "down" else (wo, 0)
            return src, [w[:, a:a + 2, D * s:D * s + D] for s in range(2)]

        def down_bank(n):
            return bank(4 + n % 2)

        XT_BANKS = ps[:, 6 * 512:8 * 512].rearrange("p (k t) -> p k t", k=KT)

        def copy_o(act, n, t):
            c, g = n // NG, n % NG
            if c and g == 0:
                act.wait_ge(s_slot, place["o", TPC * c - 1])
            act.wait_ge(s_pv, t)
            act.activation(oT[:, g, :], bank(3), ACT.Copy).then_inc(s_o, 1)

        @block.scalar
        def _(act):
            for k in range(NCH):
                if k == 1:
                    act.wait_ge(s_packed[1], 16)
                act.dma_start(xres[:, TPC * D * k:TPC * D * (k + 1)].rearrange("p (n d) -> p n d", d=D),
                              x[0, CT * k:CT * (k + 1), :].rearrange("(n p) d -> p n d", p=P)).then_inc(s_x[k], 16)
            act.sem_inc(s_gelu, 1)

            def weights_high(k):
                src, (high, _) = group_banks(k)
                act.wait_ge(s_wt, k + 1)
                act.activation(high, src, ACT.Copy).then_inc(s_wh, 1)

            def x_high(job, buf=0):
                act.wait_ge(s_xt, job + 1)
                act.activation(xT[:, buf, 0, :, :], XT_BANKS, ACT.Copy).then_inc(s_xh, 1)

            def ffn_chunk(cc, job, first=False):
                for n in range(NT):
                    act.wait_ge(s_gate, cc * NT + (n + 1))
                    act.wait_ge(s_prod, cc * NT + (1 if n < 3 else n - 1))
                    act.activation(gelu_ring[:, n % 3, :], bank(n % 2), ACT.Gelu_apprx_tanh,
                                   scale=gelu_in[:, 0:1]).then_inc(s_gelu, 1)
                    for k in behind[n] if first else ():
                        weights_high(k)
                if job is not None:
                    x_high(job)

            for k in range(2 * FIRST_PIECES):
                weights_high(k)
                if k == 3:
                    x_high(0)
            ffn_chunk(0, 1, first=True)
            with act.Fori(1, NCH - 1) as c:
                ffn_chunk(c, c + 1)
            ffn_chunk(NCH - 1, NCH)

            for c in range(NCH):
                if c >= 2:
                    act.wait_ge(s_qk_out, 16 * (c - 1))
                for m in range(4):
                    act.wait_ge(s_qk_ps, 4 * c + m + 1)
                    act.activation(qk_flat[:, c % 2, 0, m, :], bank(m % 2), ACT.Copy,
                                   scale=s_qk[:, 0:1]).then_inc(s_qkh, 1)
                if c < NCH - 1:
                    x_high(NCH + c + 1, (c + 1) % 2)
                for n in range(TPC):
                    act.wait_ge(s_v_ps, TPC * c + n + 1)
                    act.activation(v1[:, TPC * c + n, :, 0:HD],
                                   bank(2 + n % 2, D).rearrange("p (h e) -> p h e", e=HD), ACT.Copy,
                                   scale=2.0 ** (V_POW - X_POW - P_POW)).then_inc(s_v, 1)

            act.wait_ge(s_qk_out, 16 * NCH)
            for t, (n, c, g, j) in enumerate(steps):
                if n and t == first_step[n]:
                    read_o = (n - 1, t)
                else:
                    read_o = None
                q0 = max(0, P * (j - TPC * c))
                for h in range(GH):
                    b = GH * t + h
                    act.wait_ge(s_score, b + 1)
                    if b >= 8:
                        act.wait_ge(s_pv, (b - 8) // GH + 1)
                    act.activation(wreg[:, b % 8, 0:CT - q0], bank(score_bank[b], CT - q0), ACT.Exp,
                                   scale=EXP_SCALE).then_inc(s_p, 1)
                if read_o is not None:
                    copy_o(act, *read_o)
            copy_o(act, NGRP - 1, len(steps))

            ffn_chunk(NCH, 2 * NCH + 1)
            with act.Fori(1, NCH - 1) as c:
                ffn_chunk(c + NCH, c + (2 * NCH + 1))
            ffn_chunk(2 * NCH - 1, None)

        @block.vector
        def _(dve):
            step = [0]

            def own(ins):
                ins.then_inc(s_dve, 1)
                step[0] += 1
                dve.wait_ge(s_dve, step[0])

            dve.sem_inc(s_prod, 1)
            dve.sem_inc(s_resid, 1)

            dve.wait_ge(s_scales, 48)
            for k, s in enumerate((sg, su, sd)):
                last = dve.tensor_reduce(amax[:, k:k + 1], s[:, :, :].rearrange("p a b -> p (a b)"), AX.X,
                                         ALU.max, apply_absolute_value=True)
            last.then_inc(s_amax, 1)

            def statistics(chunk, n):
                dve.bn_stats(stats[:, n, :], xres[:, bass.ds(chunk * (TPC * D) + n * D, D)]).then_inc(s_dve, 1)

            def aggregate():
                for n in range(TPC):
                    last = dve.bn_aggr(mv[:, n, :], stats[:, n, :])
                last.then_inc(s_stats, 1)

            def weights_low(k):
                src, (high, low) = group_banks(k)
                dve.wait_ge(s_wh, k + 1)
                dve.tensor_tensor(low, src, high, ALU.subtract).then_inc(s_wl, 1)

            def decode(n):
                m, q = pieces[n]
                if q == 0:
                    dve.wait_ge(s_packed[m], 16)
                nat = (gate_nat, up_nat, down_nat)[m]
                if m < 2:
                    w = nat[:, 512 * q:512 * q + 512]
                else:
                    w = nat.rearrange("p (k c) -> p k c", k=KT)[:, :, 256 * q:256 * q + 256]

                def like(t):
                    return t if m < 2 else t.rearrange("p (k c) -> p k c", k=KT)

                if n >= 2:
                    dve.wait_ge(s_vals, n - 1)
                for k in range(2):
                    dve.tensor_scalar(like(code_pair[n % 2][k]), w, 28 - 4 * k, 3, ALU.logical_shift_left,
                                      ALU.arith_shift_right).then_inc(s_dve, 1)
                for k in range(2):
                    step[0] += 1
                    dve.wait_ge(s_dve, step[0])
                    c = code_pair[n % 2][k]
                    last = dve.tensor_scalar(c, c, -0x72000000, None, ALU.bitwise_and)
                last.then_inc(s_code, 1)

            def powers(cols, power):
                r, i = pow_r[:, cols], pow_i[:, cols]
                own(dve.tensor_scalar(r, amax_all[:, cols], 2.0 ** -60, None, ALU.max))
                own(dve.tensor_scalar(r.bitcast(i32), r.bitcast(i32), 0x7F800000, None, ALU.bitwise_and))
                own(dve.tensor_scalar(i.bitcast(i32), r.bitcast(i32), -1.0, float(254 << 23), ALU.mult, ALU.add))
                own(dve.tensor_scalar(mul_w[:, cols], i, 2.0 ** power, None, ALU.mult))

            dve.wait_ge(s_amax_all, 1)
            powers(slice(0, 3), W_POW + FP4_POW)
            for k, s in enumerate((sg, su, sd)):
                last = dve.tensor_scalar(s[:, :, :], s[:, :, :], mul_w[:, k:k + 1], None, ALU.mult)
            last.then_inc(s_scaled, 1)
            decode(0)
            dve.wait_ge(s_x[0], 16)
            for n in range(TPC):
                statistics(0, n)
            step[0] += TPC
            dve.wait_ge(s_dve, step[0])
            aggregate()
            decode(1)
            dve.tensor_scalar(kappa[:, :], pow_i[:, 0:1], 2.0 ** (I_POW - X_POW - W_POW), None, ALU.mult)
            dve.tensor_scalar(gelu_in[:, :], pow_r[:, 0:1], 2.0 ** (-X_POW - W_POW), None, ALU.mult)
            own(dve.tensor_scalar(tmp1[:, :], pow_r[:, 0:1], pow_r[:, 1:2], 0.5 * 2.0 ** (-I_POW - W_POW),
                                  ALU.mult, ALU.mult))
            own(dve.tensor_scalar(s_down[:, :], tmp1[:, :], pow_r[:, 2:3], None, ALU.mult))

            def projections_powers():
                dve.wait_ge(s_amax_all, 2)
                powers(slice(3, 5), P_POW)
                dve.tensor_scalar(s_qk[:, :], pow_r[:, 3:4], 2.0 ** (-X_POW - P_POW), None, ALU.mult)
                dve.tensor_scalar(s_out[:, :], pow_r[:, 3:4], pow_r[:, 4:5], 2.0 ** (-V_POW - P_POW),
                                  ALU.mult, ALU.mult).then_inc(s_scaled, 1)

            def x_low(job, buf=0):
                dve.wait_ge(s_xh, job + 1)
                dve.tensor_tensor(xT[:, buf, 1, :, :], XT_BANKS, xT[:, buf, 0, :, :], ALU.subtract).then_inc(s_xl, 1)

            FFN_STEPS = TPC

            def ffn_chunk(cc, c, job, chunk, base=None, first=False, rest=()):
                def low(n):
                    if first:
                        return
                    dve.wait_ge(s_ihigh, cc * NT + (n + 1))
                    dve.tensor_tensor(inter[:, 1, n, :], prod_ring[:, n % 3, :], inter[:, 0, n, :],
                                      ALU.subtract).then_inc(s_inter, 1)

                dve.wait_ge(s_down_done, cc * TPC + 1)
                for n in range(NT):
                    if n >= 3:
                        dve.wait_ge(s_inter, cc * NT + (n - 2))
                    dve.wait_ge(s_up, cc * NT + (n + 1))
                    dve.wait_ge(s_gelu, cc * NT + (n + 2))
                    dve.scalar_tensor_tensor(out=prod_ring[:, n % 3, :], in0=bank(2 + n % 2),
                                             scalar=kappa[:, 0:1], in1=gelu_ring[:, n % 3, :],
                                             op0=ALU.mult, op1=ALU.mult).then_inc(s_prod, 1)
                    if job is not None and n == 4 + TPC:
                        dve.wait_ge(s_dve, step[0] if base is None else base + TPC)
                    if n:
                        low(n - 1)
                    dve.wait_ge(s_prod, cc * NT + (n + 2))
                    dve.tensor_copy(inter[:, 0, n, :], prod_ring[:, n % 3, :]).then_inc(s_ihigh, 1)
                    if job is not None and 4 <= n < 4 + TPC:
                        if n == 4:
                            dve.wait_ge(s_yn, job)
                        statistics(chunk, n - 4)
                        if base is None:
                            step[0] += 1
                    if job is not None and n == 4 + TPC:
                        aggregate()
                    for u in rest[n:n + 1]:
                        maxima(*u)
                    if first:
                        if behind[n] and behind[n][0] // 2 + DECODE_AHEAD < 3 * NPIECE:
                            decode(behind[n][0] // 2 + DECODE_AHEAD)
                        if n == POWER_TILE:
                            projections_powers()
                        for k in behind[n]:
                            weights_low(k)
                low(NT - 1)
                if job is not None:
                    x_low(job)
                for n in range(TPC):
                    dve.wait_ge(s_down_done, cc * TPC + (n + 2))
                    dst = xres[:, bass.ds(c * (TPC * D) + n * D, D)]
                    dve.scalar_tensor_tensor(out=half_sum[:, n % 2, :], in0=down_bank(n)[:, D:2 * D],
                                             scalar=s_down[:, 0:1], in1=dst, op0=ALU.mult,
                                             op1=ALU.add).then_inc(s_half, 1)
                    dve.wait_ge(s_half, cc * TPC + (n + 1))
                    dve.scalar_tensor_tensor(out=dst, in0=down_bank(n)[:, 0:D], scalar=s_down[:, 0:1],
                                             in1=half_sum[:, n % 2, :], op0=ALU.mult,
                                             op1=ALU.add).then_inc(s_resid, 1)

            decode(2)
            weights_low(0)
            weights_low(1)
            decode(3)
            weights_low(2)
            weights_low(3)
            x_low(0)
            decode(4)
            dve.wait_ge(s_proj_in, 16)
            dve.tensor_reduce(amax[:, 3:4], proj_nat, AX.X, ALU.max, apply_absolute_value=True)
            dve.wait_ge(s_out_in, 16)
            dve.tensor_reduce(amax[:, 4:5], out_nat, AX.X, ALU.max,
                              apply_absolute_value=True).then_inc(s_amax, 1)
            decode(5)
            for k in range(1, NCH):
                dve.wait_ge(s_x[k], 16)
            ffn_chunk(0, 0, 1, 1, first=True)
            with dve.Fori(1, NCH - 1) as c:
                ffn_chunk(c, c, c + 1, c + 1, (c - 1) * FFN_STEPS + step[0])
            step[0] += FFN_STEPS * (NCH - 2)
            ffn_chunk(NCH - 1, NCH - 1, NCH, 0, step[0])
            step[0] += FFN_STEPS

            slot, read = [0], [0]

            def maxima(kind, n, unit):
                c, r = n // NG, n % 2
                at = 4 + 2 * (slot[0] % 2)
                if kind == "statistics":
                    dve.wait_ge(s_slot_read, place["project", TPC - 1])
                    for k in range(TPC):
                        statistics(0, k)
                    step[0] += TPC
                    dve.wait_ge(s_dve, step[0])
                    aggregate()
                    return
                if kind == "negate":
                    dve.wait_ge(s_slot_read, read[0])
                    m = m_part[:, r, 0, :]
                    if c >= 2:
                        own(dve.tensor_tensor(m, m, m_part[:, r, 1, :], ALU.max))
                    m = m.rearrange("p (a k) -> p a k", a=2)
                    own(dve.tensor_scalar(m_split[:, r, :, 0, :], m, -1.0 / MSCALE, None, ALU.mult))
                    dve.scalar_tensor_tensor(out=m_split[:, r, :, 1, :], in0=m, scalar=-1.0 / MSCALE,
                                             in1=m_split[:, r, :, 0, :], op0=ALU.mult,
                                             op1=ALU.subtract).then_inc(s_mneg, 1)
                    return
                dve.wait_ge(s_slot, slot[0] + 1)
                if kind == "o":
                    o = bank(at).rearrange("p (h e) -> p h e", e=32)
                    own(dve.reciprocal(recip[:, r, :], o[:, :, HD]))
                    dve.tensor_tensor(att[:, r, :].rearrange("p (h e) -> p h e", e=HD), o[:, :, 0:HD],
                                      recip[:, r, :].unsqueeze(2).to_broadcast([P, HEADS, HD]), ALU.mult)\
                       .then_inc(s_slot_read, 1)
                elif kind == "split":
                    src = bank(at, D).rearrange("p (k t) -> p k t", k=KT)
                    own(dve.tensor_copy(attT[:, r, 0, :, :], src))
                    dve.tensor_tensor(attT[:, r, 1, :, :], src, attT[:, r, 0, :, :], ALU.subtract)\
                       .then_inc(s_slot_read, 1)
                elif kind == "project":
                    dst = xres[:, D * n:D * n + D]
                    own(dve.scalar_tensor_tensor(out=half_sum[:, r, :], in0=bank(at, D, D), scalar=s_out[:, 0:1],
                                                 in1=dst, op0=ALU.mult, op1=ALU.add))
                    dve.scalar_tensor_tensor(out=dst, in0=bank(at, D), scalar=s_out[:, 0:1],
                                             in1=half_sum[:, r, :], op0=ALU.mult,
                                             op1=ALU.add).then_inc(s_slot_read, 1)
                elif kind == "transpose":
                    src = ps[:, 512 * at:512 * at + 1024].rearrange("p (k t) -> p k t", k=KT)
                    dve.sem_inc(s_xt, 1)
                    dve.tensor_copy(xT[:, 0, 0, :, :], src).then_inc(s_xh, 1)
                    dve.wait_ge(s_xh, n + 1)
                    dve.tensor_tensor(xT[:, 0, 1, :, :], src, xT[:, 0, 0, :, :], ALU.subtract)\
                       .then_inc(s_slot_read, 1)
                    dve.wait_ge(s_slot_read, place[kind, n])
                    dve.sem_inc(s_xl, 1)
                elif kind == "rows":
                    if n >= 2:
                        dve.wait_ge(s_mdma[r], 16 * 2 * (n // 2))
                    dve.tensor_copy(m_rows[:, r, :], ps[0:32, 512 * at:512 * at + P // 2].bitcast(f16))\
                       .then_inc(s_slot_read, 1)
                else:
                    _, width, (part, q, h, cnt) = unit
                    if cnt == 2:
                        src = ps[:, 512 * at:512 * at + 1024].rearrange("p (a n) -> p a n", a=2)[:, :, 0:width]
                    else:
                        src = ps[:, 512 * at:512 * at + width].rearrange("p (a n) -> p a n", a=1)
                    col = 8 * (h % 2) + TPC * (h // 2) + q
                    dve.tensor_reduce(m_part[:, r, part, col:col + 8 * (cnt - 1) + 1:8], src, AX.X, ALU.max)\
                       .then_inc(s_slot_read, 1)
                    read[0] = slot[0] + 1
                slot[0] += 1

            for c in range(NCH):
                if c < NCH - 1:
                    dve.wait_ge(s_yn, NCH + c + 1)
                    for n in range(TPC):
                        statistics(c + 1, n)
                    step[0] += TPC
                    dve.wait_ge(s_dve, step[0])
                    aggregate()
                for m in range(4):
                    dve.wait_ge(s_qkh, 4 * c + m + 1)
                    dve.scalar_tensor_tensor(out=qk_flat[:, c % 2, 1, m, :], in0=bank(m % 2), scalar=s_qk[:, 0:1],
                                             in1=qk_flat[:, c % 2, 0, m, :], op0=ALU.mult,
                                             op1=ALU.subtract).then_inc(s_qkl, 1)
                    if c == NCH - 1:
                        for u in early[m]:
                            maxima(*u)
                if c < NCH - 1:
                    x_low(NCH + c + 1, (c + 1) % 2)

            for k in range(4, 4 + TPC):
                for u in early[k]:
                    maxima(*u)
            dve.wait_ge(s_v, TT)
            dve.memset(bank(3), 0.0).then_inc(s_o, 1)
            for t in range(len(steps)):
                for u in plan[t]:
                    maxima(*u)

            dve.wait_ge(s_slot_read, len(in_slots) - len(plan[len(steps)]))
            ffn_chunk(NCH, 0, 2 * NCH + 1, 1, rest=plan[len(steps)])
            dve.wait_ge(s_slot_read, len(in_slots))
            with dve.Fori(1, NCH - 1) as c:
                ffn_chunk(c + NCH, c, c + (2 * NCH + 1), c + 1, (c - 1) * FFN_STEPS + step[0])
            ffn_chunk(2 * NCH - 1, NCH - 1, None, None, None)

        @block.tensor
        def _(pe):
            pe.sem_inc(s_down_done, 1)
            pe.wait_ge(s_const, 1)

            def transpose_weights(k):
                kind, j = groups[k]
                dst = w_bank(k)
                if kind in ("gate", "up", "down"):
                    n = k // 2
                    pe.wait_ge(s_vals, n + 1)
                else:
                    pe.wait_ge(s_scaled, 3)
                if k >= W_BANKS:
                    pe.wait_ge(s_wl, k - W_BANKS + 1)
                for a in range(2):
                    for kt in range(KT):
                        if kind in ("gate", "up"):
                            v = vals[n % 4].rearrange("p (r k j) -> p r k j", r=4, k=2)
                            src, at = v[:, 2 * (j % 2) + a, kt, :], D * kt + P * a
                        elif kind == "down":
                            v = vals[n % 4].rearrange("p (r k j) -> p r k j", r=2, k=2)
                            src, at = v[:, a, kt, P * (j % 2):P * (j % 2) + P], D * kt + P * a
                        elif kind == "proj":
                            v = proj_nat.rearrange("p (m j k) -> p m j k", m=6, k=2)
                            src, at = v[:, 2 * j + a, :, kt], D * kt + P * a
                        else:
                            v = out_nat.rearrange("p (m k j) -> p m k j", m=2, k=2)
                            src, at = v[:, a, kt, :], D * kt + P * a
                        last = pe.transpose(dst[:, at:at + P], src, ident[:, :])
                last.then_inc(s_wt, 1)

            def transpose_x(job):
                pe.wait_ge(s_yn, job + 1)
                for n in range(TPC):
                    v = yn[:, n, :].rearrange("p (j k) -> p j k", k=KT)
                    for kt in range(KT):
                        last = pe.transpose(XT_BANKS[:, kt, P * n:P * n + P], v[:, :, kt], ident[:, :])
                last.then_inc(s_xt, 1)

            def three_passes(dst, w, cols, buf=0):
                for kt in range(KT):
                    pe.matmul(dst, w[:, 0, kt, cols], xT[:, buf, 0, kt, :], start=(kt == 0), stop=False)
                    pe.matmul(dst, w[:, 0, kt, cols], xT[:, buf, 1, kt, :], start=False, stop=False)
                    last = pe.matmul(dst, w[:, 1, kt, cols], xT[:, buf, 0, kt, :], start=False, stop=(kt == KT - 1))
                return last

            def ffn_chunk(cc, job_here, job, first=False, rest=()):
                pe.wait_ge(s_xl, job_here + 1)
                for n in range(NT):
                    cols = slice(P * n, P * n + P)
                    if first:
                        pe.wait_ge(s_wl, groups.index(("up", n // 2)) + 1)
                    pe.wait_ge(s_gelu, cc * NT + (1 if n < 2 else n))
                    three_passes(bank(n % 2), wg, cols).then_inc(s_gate, 1)
                    pe.wait_ge(s_prod, cc * NT + (1 if n < 2 else n))
                    three_passes(bank(2 + n % 2), wu, cols).then_inc(s_up, 1)
                    for k in behind[n] if first else ():
                        transpose_weights(k)
                    for u in rest[n:n + 1]:
                        planned(*u)
                if rest:
                    pe.wait_ge(s_slot_read, len(in_slots))
                if job is not None:
                    transpose_x(job)
                if first:
                    pe.wait_ge(s_wl, len(groups))
                for m in range(TPC):
                    pe.wait_ge(s_resid, cc * TPC + (1 if m < 2 else m))
                    tok = slice(P * m, P * m + P)
                    for n in range(NT):
                        if m == 0:
                            pe.wait_ge(s_inter, cc * NT + (n + 1))
                        pe.matmul(down_bank(m), inter[:, 0, n, tok], wd[:, n, :], start=(n == 0), stop=False)
                        last = pe.matmul(down_bank(m)[:, 0:D], inter[:, 1, n, tok], wd[:, n, 0:D],
                                         start=False, stop=(n == NT - 1))
                    last.then_inc(s_down_done, 1)

            for k in range(2 * FIRST_PIECES):
                transpose_weights(k)
                if k == 3:
                    transpose_x(0)
            ffn_chunk(0, 0, 1, first=True)
            with pe.Fori(1, NCH - 1) as c:
                ffn_chunk(c, c, c + 1)
            ffn_chunk(NCH - 1, NCH - 1, NCH)

            slot = [0]

            def planned(kind, n, unit):
                if kind in ("negate", "statistics"):
                    return
                c, g = n // NG, n % NG
                at = 4 + 2 * (slot[0] % 2)
                if slot[0] >= 2:
                    pe.wait_ge(s_slot_read, slot[0] - 1)
                if kind == "o":
                    i, q = n // TPC, n % TPC
                    pe.wait_ge(s_o, 1 + NG * (i + 1))
                    for g in range(NG):
                        last = pe.transpose(bank(at, P, P * g), oT[:, g, P * q:P * q + P], ident[:, :])
                elif kind == "split":
                    pe.wait_ge(s_slot_read, place["o", n])
                    for kt in range(KT):
                        last = pe.transpose(bank(at, P, P * kt), att[:, n % 2, P * kt:P * kt + P], ident[:, :])
                elif kind == "project":
                    pe.wait_ge(s_slot_read, place["split", n])
                    for kt in range(KT):
                        pe.matmul(bank(at), attT[:, n % 2, 0, kt, :], wo[:, kt, :], start=(kt == 0), stop=False)
                        last = pe.matmul(bank(at, D), attT[:, n % 2, 1, kt, :], wo[:, kt, 0:D],
                                         start=False, stop=(kt == KT - 1))
                elif kind == "transpose":
                    pe.wait_ge(s_yn, n + 1)
                    for m in range(TPC):
                        v = yn[:, m, :].rearrange("p (j k) -> p j k", k=KT)
                        for kt in range(KT):
                            last = pe.transpose(bank(at + kt, P, P * m), v[:, :, kt], ident[:, :])
                elif kind == "rows":
                    pe.wait_ge(s_mneg, n + 1)
                    last = pe.transpose(ps[0:32, 512 * at:512 * at + P // 2].bitcast(f16),
                                        m_split[:, n % 2, :, :, :].rearrange("p a s k -> p (a s k)"), ident16[:, :])
                else:
                    if g == 0 and unit[2][1:3] == (0, 0) and unit[2][0] == 0:
                        pe.wait_ge(s_kstack[c], 16 * 6)
                        pe.wait_ge(s_qstack[c], 16 * (6 if c < 2 else 8))
                    for k, (h, i, k0, k1) in enumerate(unit[0]):
                        pair = 2 * g + h // 2
                        for m in range(k0, k1, 512):
                            w = min(512, k1 - m)
                            dst = bank(at + k + (m - k0) // 512, w)
                            diag = P * i - m
                            q0 = P * (i - TPC * c)
                            last = pe.matmul(dst, qreg[:, c % 2, h % 2, pair, q0:q0 + P], kreg[:, pair, m:m + w],
                                             start=True, stop=not 0 <= diag < w)
                            if 0 <= diag < w:
                                last = masked(dst[:, diag:diag + P], tri_a)
                last.then_inc(s_slot, 1)
                slot[0] += 1

            def masked(dst, tri):
                return pe.matmul(dst, tri[:, :], big_id[:, :], start=False, stop=True)

            def scores(t, h):
                n, c, g, j = steps[t]
                b = GH * t + h
                if last_in_bank[b] is not None:
                    pe.wait_ge(s_p, last_in_bank[b] + 1)
                elif score_bank[b] > 3:
                    pe.wait_ge(s_slot_read, len(in_slots) - len(plan[len(steps)]))
                pair = 2 * g + h // 2
                q0 = max(0, P * (j - TPC * c))
                dst = bank(score_bank[b], CT - q0)
                diag = j >= TPC * c
                last = pe.matmul(dst, kreg[:, pair, P * j:P * j + P], qreg[:, c % 2, h % 2, pair, q0:CT],
                                 start=True, stop=not diag)
                if diag:
                    last = masked(dst[:, 0:P], tri_b)
                last.then_inc(s_score, 1)

            def weighted_values(t):
                n, c, g, j = steps[t]
                q0 = max(0, P * (j - TPC * c))
                if j == 0:
                    pe.wait_ge(s_o, n + 1)
                for h in range(GH):
                    b = GH * t + h
                    pe.wait_ge(s_p, b + 1)
                    last = pe.matmul(bank(3, CT - q0, q0)[32 * h:32 * h + HD + 1, :], v1[:, j, GH * g + h, :],
                                     wreg[:, b % 8, 0:CT - q0], start=(j == 0), stop=(j == TPC * (c + 1) - 1))
                last.then_inc(s_pv, 1)

            for c in range(NCH):
                pe.wait_ge(s_xl, NCH + c + 1)
                if c == NCH - 1:
                    pe.wait_ge(s_const, 2)
                    pe.wait_ge(s_resid, 1 + TPC * NCH)
                for m in range(4):
                    if 4 * c + m >= 2:
                        pe.wait_ge(s_qkl, 4 * c + m - 1)
                    three_passes(bank(m % 2), wp, slice(P * m, P * m + P), c % 2).then_inc(s_qk_ps, 1)
                    if c == NCH - 1:
                        for u in early[m]:
                            planned(*u)
                if c < NCH - 1:
                    transpose_x(NCH + c + 1)
                for n in range(TPC):
                    if TPC * c + n >= 2:
                        pe.wait_ge(s_v, TPC * c + n - 1)
                    dst, tok = bank(2 + n % 2, D), slice(P * n, P * n + P)
                    for kt in range(KT):
                        cols = slice(2 * D, 3 * D)
                        pe.matmul(dst, xT[:, c % 2, 0, kt, tok], wp[:, 0, kt, cols], start=(kt == 0), stop=False)
                        pe.matmul(dst, xT[:, c % 2, 0, kt, tok], wp[:, 1, kt, cols], start=False, stop=False)
                        last = pe.matmul(dst, xT[:, c % 2, 1, kt, tok], wp[:, 0, kt, cols], start=False,
                                         stop=(kt == KT - 1))
                    last.then_inc(s_v_ps, 1)
                    if c == NCH - 1:
                        for u in early[4 + n]:
                            planned(*u)

            pe.wait_ge(s_qkl, 4 * NCH)
            pe.wait_ge(s_v, TT)
            for t in range(len(steps)):
                if t == first_step[steps[t][0]]:
                    n = steps[t][0]
                    pe.wait_ge(s_mdma[n % 2], 16 * 2 * (n // 2 + 1))
                parts = [lambda: (scores(t, 0), scores(t, 1)), lambda: scores(t, 2), lambda: scores(t, 3)]
                if t:
                    parts.insert(2, lambda: weighted_values(t - 1))
                for k, part in enumerate(parts):
                    part()
                    for u in plan[t][len(plan[t]) * k // len(parts):len(plan[t]) * (k + 1) // len(parts)]:
                        planned(*u)
            weighted_values(len(steps) - 1)

            pe.wait_ge(s_p, GH * len(steps))
            pe.wait_ge(s_o, 1 + NGRP)
            ffn_chunk(NCH, 2 * NCH, 2 * NCH + 1, rest=plan[len(steps)])
            with pe.Fori(1, NCH - 1) as c:
                ffn_chunk(c + NCH, c + 2 * NCH, c + (2 * NCH + 1))
            ffn_chunk(2 * NCH - 1, 3 * NCH - 1, None)


_INS = ["L0_attn_x", "L0_attn_w_project", "L0_attn_w_out", "L0_ffn_gate_W_packed", "L0_ffn_gate_scales",
        "L0_ffn_up_W_packed", "L0_ffn_up_scales", "L0_ffn_down_W_packed", "L0_ffn_down_scales"]


def kernel(**inputs):
    import numpy as _np
    import concourse.bacc as _bacc
    from concourse import mybir as _mybir
    from concourse.bass_utils import run_bass_kernel_spmd as _run

    nc = _bacc.Bacc("TRN2", target_bir_lowering=False, num_devices=1)
    arrays, args = {}, []
    for name in _INS:
        a = _np.ascontiguousarray(inputs[name])
        arrays[f"in_{name}"] = a
        args.append(nc.dram_tensor(f"in_{name}", a.shape, _mybir.dt.from_np(a.dtype), kind="ExternalInput").ap())
    shape = inputs["L0_attn_x"].shape
    args.append(nc.dram_tensor("out_x", shape, _mybir.dt.float32, kind="ExternalOutput").ap())
    macaron_block(nc, *args)
    r = _run(nc, [arrays], core_ids=[0])
    return r.results[0]["out_x"]
```
